# Optimizing a Trainium2 kernel written in Bass

```python
import numpy as np
import jax
import jax.numpy as jnp

def _softmax(x, axis=-1):
    return jax.nn.softmax(x, axis=axis)

def _gelu(x):
    return jax.nn.gelu(x, approximate=True)

def _silu(x):
    return jax.nn.silu(x)

def _sigmoid(x):
    return jax.nn.sigmoid(x)

def _layernorm(x, axis=-1, eps=1e-05):
    m = jnp.mean(x, axis=axis, keepdims=True)
    v = jnp.var(x, axis=axis, keepdims=True)
    return (x - m) / jnp.sqrt(v + eps)

def _scatter_add(tgt, idx, src, axis=0):
    return tgt.at[idx].add(src)

def _segment_sum(src, seg, n):
    return jax.ops.segment_sum(src, seg, n)
kernel_name = 'mk_dlrm_tower_d1_rec_r8_75a49c'

def setup_inputs(seed: int=0):
    np.random.seed(seed)
    _w = jnp.asarray

    def _rec_inputs():
        import jax
        import jax.numpy as jnp
        _tk = jax.random.key(seed)
        dense_ctx = jax.random.normal(jax.random.fold_in(_tk, 190), (1024, 16), jnp.float32)
        ids = jnp.stack([jax.random.randint(jax.random.fold_in(_tk, 200 + f), (1024,), 0, v, jnp.int32) for f, v in enumerate([12500, 1250, 1250, 125000, 1000, 125000, 125000, 1000, 12500, 1000, 1000, 125000, 12500, 12500, 1000, 125000, 125000, 1000, 1000, 1250, 125000, 1000, 12500, 1000, 12500, 1000])], axis=1)
        tbl_0 = 0.05 * jax.random.normal(jax.random.fold_in(_tk, 500 + 0), (12500, 32), jnp.float32)
        tbl_1 = 0.05 * jax.random.normal(jax.random.fold_in(_tk, 500 + 1), (1250, 32), jnp.float32)
        tbl_2 = 0.05 * jax.random.normal(jax.random.fold_in(_tk, 500 + 2), (1250, 32), jnp.float32)
        tbl_3 = 0.05 * jax.random.normal(jax.random.fold_in(_tk, 500 + 3), (125000, 32), jnp.float32)
        tbl_4 = 0.05 * jax.random.normal(jax.random.fold_in(_tk, 500 + 4), (1000, 32), jnp.float32)
        tbl_5 = 0.05 * jax.random.normal(jax.random.fold_in(_tk, 500 + 5), (125000, 32), jnp.float32)
        tbl_6 = 0.05 * jax.random.normal(jax.random.fold_in(_tk, 500 + 6), (125000, 32), jnp.float32)
        tbl_7 = 0.05 * jax.random.normal(jax.random.fold_in(_tk, 500 + 7), (1000, 32), jnp.float32)
        tbl_8 = 0.05 * jax.random.normal(jax.random.fold_in(_tk, 500 + 8), (12500, 32), jnp.float32)
        tbl_9 = 0.05 * jax.random.normal(jax.random.fold_in(_tk, 500 + 9), (1000, 32), jnp.float32)
        tbl_10 = 0.05 * jax.random.normal(jax.random.fold_in(_tk, 500 + 10), (1000, 32), jnp.float32)
        tbl_11 = 0.05 * jax.random.normal(jax.random.fold_in(_tk, 500 + 11), (125000, 32), jnp.float32)
        tbl_12 = 0.05 * jax.random.normal(jax.random.fold_in(_tk, 500 + 12), (12500, 32), jnp.float32)
        tbl_13 = 0.05 * jax.random.normal(jax.random.fold_in(_tk, 500 + 13), (12500, 32), jnp.float32)
        tbl_14 = 0.05 * jax.random.normal(jax.random.fold_in(_tk, 500 + 14), (1000, 32), jnp.float32)
        tbl_15 = 0.05 * jax.random.normal(jax.random.fold_in(_tk, 500 + 15), (125000, 32), jnp.float32)
        tbl_16 = 0.05 * jax.random.normal(jax.random.fold_in(_tk, 500 + 16), (125000, 32), jnp.float32)
        tbl_17 = 0.05 * jax.random.normal(jax.random.fold_in(_tk, 500 + 17), (1000, 32), jnp.float32)
        tbl_18 = 0.05 * jax.random.normal(jax.random.fold_in(_tk, 500 + 18), (1000, 32), jnp.float32)
        tbl_19 = 0.05 * jax.random.normal(jax.random.fold_in(_tk, 500 + 19), (1250, 32), jnp.float32)
        tbl_20 = 0.05 * jax.random.normal(jax.random.fold_in(_tk, 500 + 20), (125000, 32), jnp.float32)
        tbl_21 = 0.05 * jax.random.normal(jax.random.fold_in(_tk, 500 + 21), (1000, 32), jnp.float32)
        tbl_22 = 0.05 * jax.random.normal(jax.random.fold_in(_tk, 500 + 22), (12500, 32), jnp.float32)
        tbl_23 = 0.05 * jax.random.normal(jax.random.fold_in(_tk, 500 + 23), (1000, 32), jnp.float32)
        tbl_24 = 0.05 * jax.random.normal(jax.random.fold_in(_tk, 500 + 24), (12500, 32), jnp.float32)
        tbl_25 = 0.05 * jax.random.normal(jax.random.fold_in(_tk, 500 + 25), (1000, 32), jnp.float32)
        _rk = jax.random.fold_in(_tk, 7)
        W_top1 = 0.0606339 * jax.random.normal(jax.random.fold_in(_tk, 801), (272, 512), jnp.float32)
        W_top2 = 0.0441942 * jax.random.normal(jax.random.fold_in(_tk, 802), (512, 256), jnp.float32)
        W_top3 = 0.0625 * jax.random.normal(jax.random.fold_in(_tk, 803), (256, 1), jnp.float32)
        b_top1 = jnp.zeros((512,), jnp.float32)
        b_top2 = jnp.zeros((256,), jnp.float32)
        return (dense_ctx, ids, tbl_0, tbl_1, tbl_2, tbl_3, tbl_4, tbl_5, tbl_6, tbl_7, tbl_8, tbl_9, tbl_10, tbl_11, tbl_12, tbl_13, tbl_14, tbl_15, tbl_16, tbl_17, tbl_18, tbl_19, tbl_20, tbl_21, tbl_22, tbl_23, tbl_24, tbl_25, W_top1, b_top1, W_top2, b_top2, W_top3)
    dense_ctx, ids, tbl_0, tbl_1, tbl_2, tbl_3, tbl_4, tbl_5, tbl_6, tbl_7, tbl_8, tbl_9, tbl_10, tbl_11, tbl_12, tbl_13, tbl_14, tbl_15, tbl_16, tbl_17, tbl_18, tbl_19, tbl_20, tbl_21, tbl_22, tbl_23, tbl_24, tbl_25, W_top1, b_top1, W_top2, b_top2, W_top3 = _rec_inputs()

    def _L0_rec_setup():
        import jax, jax.numpy as jnp
        import numpy as np
        M_FIELDS = 26
        H1 = 128
        H2 = 128
        BATCH = 256
        EMB_K = 32

        def _cin_layer(x_prev, x0, W, b):
            return jnp.einsum('bik,bjk,hij->bhk', x_prev, x0, W) + b[None, :, None]
        key = jax.random.key(seed)
        k0, k1, k2, k3, k4 = jax.random.split(key, 5)
        inputs = jax.random.normal(k0, (BATCH, M_FIELDS, EMB_K), dtype=jnp.float32)
        W1 = jax.random.normal(k1, (H1, M_FIELDS, M_FIELDS), dtype=jnp.float32) * 0.05
        b1 = jax.random.normal(k2, (H1,), dtype=jnp.float32) * 0.05
        W2 = jax.random.normal(k3, (H2, H1, M_FIELDS), dtype=jnp.float32) * 0.05
        b2 = jax.random.normal(k4, (H2,), dtype=jnp.float32) * 0.05
        return {'inputs': inputs, 'W1': W1, 'b1': b1, 'W2': W2, 'b2': b2}
    _L0_rec_all = _L0_rec_setup()
    _L0_rec_in = {k: v for k, v in _L0_rec_all.items() if k in ('W1', 'b1', 'W2', 'b2')}
    del _L0_rec_all
    return {'dense_ctx': dense_ctx, 'ids': ids, 'tbl_0': tbl_0, 'tbl_1': tbl_1, 'tbl_2': tbl_2, 'tbl_3': tbl_3, 'tbl_4': tbl_4, 'tbl_5': tbl_5, 'tbl_6': tbl_6, 'tbl_7': tbl_7, 'tbl_8': tbl_8, 'tbl_9': tbl_9, 'tbl_10': tbl_10, 'tbl_11': tbl_11, 'tbl_12': tbl_12, 'tbl_13': tbl_13, 'tbl_14': tbl_14, 'tbl_15': tbl_15, 'tbl_16': tbl_16, 'tbl_17': tbl_17, 'tbl_18': tbl_18, 'tbl_19': tbl_19, 'tbl_20': tbl_20, 'tbl_21': tbl_21, 'tbl_22': tbl_22, 'tbl_23': tbl_23, 'tbl_24': tbl_24, 'tbl_25': tbl_25, 'W_top1': W_top1, 'b_top1': b_top1, 'W_top2': W_top2, 'b_top2': b_top2, 'W_top3': W_top3, 'L0_rec_W1': _L0_rec_in['W1'], 'L0_rec_b1': _L0_rec_in['b1'], 'L0_rec_W2': _L0_rec_in['W2'], 'L0_rec_b2': _L0_rec_in['b2']}

def reference(dense_ctx, ids, tbl_0, tbl_1, tbl_2, tbl_3, tbl_4, tbl_5, tbl_6, tbl_7, tbl_8, tbl_9, tbl_10, tbl_11, tbl_12, tbl_13, tbl_14, tbl_15, tbl_16, tbl_17, tbl_18, tbl_19, tbl_20, tbl_21, tbl_22, tbl_23, tbl_24, tbl_25, W_top1, b_top1, W_top2, b_top2, W_top3, L0_rec_W1, L0_rec_b1, L0_rec_W2, L0_rec_b2):
    import jax
    import jax.numpy as jnp

    def _L0_rec_ref(inputs, W1, b1, W2, b2):
        import jax, jax.numpy as jnp
        import numpy as np
        M_FIELDS = 26
        H1 = 128
        H2 = 128
        BATCH = 256
        EMB_K = 32

        def _cin_layer(x_prev, x0, W, b):
            return jnp.einsum('bik,bjk,hij->bhk', x_prev, x0, W) + b[None, :, None]
        x1 = _cin_layer(inputs, inputs, W1, b1)
        x2 = _cin_layer(x1, inputs, W2, b2)
        res = jnp.concatenate([x1, x2], axis=1)
        return jnp.sum(res, axis=-1)
    e = jnp.stack([tbl_0[ids[:, 0]], tbl_1[ids[:, 1]], tbl_2[ids[:, 2]], tbl_3[ids[:, 3]], tbl_4[ids[:, 4]], tbl_5[ids[:, 5]], tbl_6[ids[:, 6]], tbl_7[ids[:, 7]], tbl_8[ids[:, 8]], tbl_9[ids[:, 9]], tbl_10[ids[:, 10]], tbl_11[ids[:, 11]], tbl_12[ids[:, 12]], tbl_13[ids[:, 13]], tbl_14[ids[:, 14]], tbl_15[ids[:, 15]], tbl_16[ids[:, 16]], tbl_17[ids[:, 17]], tbl_18[ids[:, 18]], tbl_19[ids[:, 19]], tbl_20[ids[:, 20]], tbl_21[ids[:, 21]], tbl_22[ids[:, 22]], tbl_23[ids[:, 23]], tbl_24[ids[:, 24]], tbl_25[ids[:, 25]]], axis=1)
    z = _L0_rec_ref(e, L0_rec_W1, L0_rec_b1, L0_rec_W2, L0_rec_b2)
    z = z.reshape(z.shape[0], -1)
    h = jnp.concatenate([z, dense_ctx], axis=1)
    h = jnp.maximum(h @ W_top1 + b_top1, 0.0)
    h = jnp.maximum(h @ W_top2 + b_top2, 0.0)
    y = h @ W_top3
    return y

_drawn_inputs = setup_inputs


def setup_inputs(seed=0):
    import zlib

    import numpy as np

    out = dict(_drawn_inputs(seed))
    spreads = {'b_top1': (0.0, 2.0), 'b_top2': (0.0, 0.8)}
    factors = {'tbl_0': 8.0,
     'tbl_1': 8.0,
     'tbl_2': 8.0,
     'tbl_3': 8.0,
     'tbl_4': 8.0,
     'tbl_5': 8.0,
     'tbl_6': 8.0,
     'tbl_7': 8.0,
     'tbl_8': 8.0,
     'tbl_9': 8.0,
     'tbl_10': 8.0,
     'tbl_11': 8.0,
     'tbl_12': 8.0,
     'tbl_13': 8.0,
     'tbl_14': 8.0,
     'tbl_15': 8.0,
     'tbl_16': 8.0,
     'tbl_17': 8.0,
     'tbl_18': 8.0,
     'tbl_19': 8.0,
     'tbl_20': 8.0,
     'tbl_21': 7.715,
     'tbl_22': 8.0,
     'tbl_23': 8.0,
     'tbl_24': 8.0,
     'tbl_25': 8.0,
     'L0_rec_W1': 8.0,
     'L0_rec_W2': 4.173,
     'dense_ctx': 5.916}
    for name, (base, spread) in spreads.items():
        noise = np.random.default_rng([zlib.crc32(name.encode()), seed]).standard_normal(out[name].shape)
        drawn = base * np.exp(spread * noise) if base else spread * noise
        out[name] = jnp.asarray(drawn.astype(out[name].dtype))
    for name, factor in factors.items():
        out[name] = (out[name] * factor).astype(out[name].dtype)
    return out
```

```python
from contextlib import ExitStack

import concourse.bass as bass
from concourse import mybir

F32 = mybir.dt.float32
I32 = mybir.dt.int32
ALU = mybir.AluOpType
ACT = mybir.ActivationFunctionType


def build_tower(nc, dense, ids, tables, w_top1, b_top1, w_top2, b_top2, w_top3, w1, b1, w2, b2, out):
    B, DC = dense.shape
    NF = len(tables)
    K = tables[0].shape[1]
    H = w1.shape[0]
    N1, N2 = w_top1.shape[1], w_top2.shape[1]
    P = 128
    Q = P // K
    GF = NF // 2
    ND = (GF + 1) // 2
    NP = GF * ND
    R = NP + 1 + GF
    UB = 16
    BT = P // Q
    HB = 512
    HALVES, TILES = B // HB, HB // P
    QUAD = 4
    RW = 2 * NP + 1 + GF * GF
    AB = 2 * NP + 1
    FX = GF + ND - 1
    GROWS = NF + GF
    GRAMS = GROWS * GF
    NG = -(-GRAMS // P)
    GC = -(-GRAMS // NG)
    G_LAST = GRAMS - (NG - 1) * GC
    C1, C2 = N1 // P, N2 // P
    FILLS_T = TILES * (BT // QUAD) * 2
    FILLS_H = FILLS_T + C1
    assert K == 32 and NG == 4 and GF % 2 == 1 and NF == 2 * GF and H == P and FILLS_H % 4 == 0

    with ExitStack() as ctx:
        def sb(name, shape, dt=F32):
            return ctx.enter_context(nc.sbuf_tensor(name, shape, dt))

        def sem(name):
            return ctx.enter_context(nc.semaphore(name))

        moments = sb("moments", [P, 2 * NF * HB])
        cubic_w = sb("cubic_w", [NP + 1, 2 * NF, H])
        pairs = sb("pairs", [P, 2, UB, 2, R])
        block_e = sb("block_e", [P, 2, UB, Q, NF])
        rows_e = sb("rows_e", [P, 2, NF * K])
        emb_t = sb("emb_t", [P, 2 * FX, BT])
        gram = sb("gram", [P, NG, HB])
        gram_w = sb("gram_w", [P, NG, H])
        wt1 = sb("wt1", [P, 3, N1])
        wt2 = sb("wt2", [P, C1, N2])
        wt3 = sb("wt3", [P, C2])
        dense_t = sb("dense_t", [DC, B])
        ids_all = sb("ids_all", [P, B // P, NF], I32)
        ids_now = sb("ids_now", [P, 2, NF], I32)
        ident = sb("ident", [P, P])
        bias1 = sb("bias1", [P, C1])
        bias2 = sb("bias2", [P, C2])
        bias_in = sb("bias_in", [P, 2])
        bias_z = sb("bias_z", [P, 2])
        y_row = gram[0:1, 0, :]

        ring = [ctx.enter_context(nc.psum_tensor(f"ring{i}", [P, 512], F32)) for i in range(4)]
        z_bank = [ctx.enter_context(nc.psum_tensor(f"z_bank{i}", [P, 512], F32)) for i in range(2)]
        h2_bank = [ctx.enter_context(nc.psum_tensor(f"h2_bank{i}", [P, 512], F32)) for i in range(2)]

        class Region:
            def __init__(self):
                self.at = 0

            def take(self, n):
                self.at += n
                return moments[:, self.at - n:self.at]

        pre = Region()
        w1_raw = pre.take(NF * NF)
        w2_raw = pre.take(H * NF)
        w2_t = pre.take(NF * H)
        w1_sym = pre.take(RW)
        gram_w_rows = pre.take(GROWS * GF)
        cin_w = pre.take(NF * RW)
        dense_rows = pre.take(B // P * DC).rearrange("p (t c) -> p t c", c=DC)
        mlp = Region()
        z_sb = mlp.take(2 * HB)
        h1_sb = mlp.take(C1 * HB)
        h2_sb = mlp.take(C2 * HB)

        def view(base, off, *dims):
            return bass.AP(base.tensor, base.offset + off, [list(base.ap[0])] + [list(d) for d in dims])

        ids_in = sem("ids_in")
        w1_in, w2_in, b_in, dense_in = sem("w1_in"), sem("w2_in"), sem("b_in"), sem("dense_in")
        mlp_w_in = sem("mlp_w_in")
        gathered = [sem("gathered0"), sem("gathered1")]
        gram_in = sem("gram_in")
        y_out = sem("y_out")
        ident0, ident_ready, ids_copied = sem("ident0"), sem("ident_ready"), sem("ids_copied")
        ids_passed = sem("ids_passed")
        slot_free = sem("slot_free")
        emb_ready = sem("emb_ready")
        unit_ready = sem("unit_ready")
        w1_sym_ready, gram_rows_ready = sem("w1_sym_ready"), sem("gram_rows_ready")
        sym_step, cin_w_ready, bias_ready = sem("sym_step"), sem("cin_w_ready"), sem("bias_ready")
        zeroed = sem("zeroed")
        unit_free = sem("unit_free")
        ring_full = sem("ring_full")
        z_full, h2_full, y_full = sem("z_full"), sem("h2_full"), sem("y_full")
        ring_drained = sem("ring_drained")
        z_ready, h2_ready, y_ready = sem("z_ready"), sem("h2_ready"), sem("y_ready")

        n_w2t = -(-NF // 4)
        n_dense = B // HB
        n_gw = 1
        n_v = 2 * NF // 4
        first_w2t = 0
        first_gw = first_w2t + n_w2t
        first_dense = first_gw + n_gw
        first_cin = first_dense + n_dense
        first_v = first_cin + NF
        first_main = first_v + n_v

        def rotations(d):
            if d == 0:
                return [(0, GF, 0)]
            return [(0, GF - d, 0), (GF - d, d, GF)]

        def gram_runs(lo, hi):
            cut = (lo // GC + 1) * GC
            return [(lo, hi)] if hi <= cut else [(lo, cut), (cut, hi)]

        UNIT_OPS = 3 + Q
        GRAM_DMAS = sum(len(gram_runs(r * GF, r * GF + GF)) for r in range(GROWS))

        block = ctx.enter_context(nc.Block())

        @block.sync
        def _(sp):
            sp.dma_start(ids_all[:], ids.rearrange("(t p) f -> p t f", p=P)).then_inc(ids_in, 16)
            sp.dma_start(w2_raw, w2.rearrange("h i l -> h (i l)")).then_inc(w2_in, 16)
            sp.dma_start(w1_raw, w1.rearrange("h i j -> h (i j)")).then_inc(w1_in, 16)
            sp.dma_start(dense_rows, dense.rearrange("(t p) c -> p t c", p=P)).then_inc(dense_in, 16)
            sp.dma_start(bias_in[:, 0:1], b1.rearrange("(h a) -> h a", a=1)).then_inc(b_in, 16)
            sp.dma_start(bias_in[:, 1:2], b2.rearrange("(h a) -> h a", a=1)).then_inc(b_in, 16)
            sp.dma_start(wt1[:, 0:2, :], w_top1[0:2 * P, :].rearrange("(c p) n -> p c n", p=P)).then_inc(mlp_w_in, 16)
            sp.dma_start(wt1[0:DC, 2, :], w_top1[2 * P:2 * P + DC, :]).then_inc(mlp_w_in, 16)
            sp.dma_start(wt2[:], w_top2.rearrange("(c p) n -> p c n", p=P)).then_inc(mlp_w_in, 16)
            with nc.allow_non_contiguous_dma(reason="small vectors onto the partitions"):
                sp.dma_start(wt3[:], w_top3.rearrange("(c p) a -> p (c a)", p=P)).then_inc(mlp_w_in, 16)
                sp.dma_start(bias1[:], b_top1.rearrange("(c p) -> p c", p=P)).then_inc(mlp_w_in, 16)
                sp.dma_start(bias2[:], b_top2.rearrange("(c p) -> p c", p=P)).then_inc(mlp_w_in, 16)
            with sp.Fori(0, HALVES) as half:
                row0 = sp.snap(half * HB)
                sp.wait_ge(ring_drained, half * FILLS_H + first_main + FILLS_T)
                for r in range(GROWS):
                    group, field = (0, r) if r < NF else (1, r - GF)
                    src = moments[NP + 1:R, (group * NF + field) * HB:(group * NF + field + 1) * HB]
                    for lo, hi in gram_runs(r * GF, r * GF + GF):
                        dst = gram[lo % GC:lo % GC + hi - lo, lo // GC, :]
                        sp.dma_start(dst, src[lo - r * GF:hi - r * GF, :]).then_inc(gram_in, 16)
                sp.wait_ge(y_ready, half + 1)
                sp.dma_start(out.rearrange("b a -> a b")[:, bass.ds(row0, HB)], y_row).then_inc(y_out, 16)
            sp.wait_ge(y_out, 16 * HALVES)

        @block.gpsimd
        def _(pool):
            nc.gpsimd.memset(ident[:], 0.0).then_inc(ident0, 1)
            pool.wait_ge(ident0, 1)
            nc.gpsimd.affine_select(out=ident[:], in_=ident[:], pattern=[[-1, P]], compare_op=ALU.not_equal,
                                    fill=1.0, base=0, channel_multiplier=1).then_inc(ident_ready, 1)
            pool.wait_ge(ids_in, 16)
            with pool.Fori(0, B // P // 2) as pair:
                for slot in range(2):
                    pool.wait_ge(slot_free, pair * 2 + slot + 1)
                    nc.gpsimd.tensor_copy(ids_now[:, slot, :], ids_all[:, bass.ds(pair * 2 + slot, 1), :]).then_inc(ids_copied, 1)
                    pool.wait_ge(ids_copied, pair * 2 + slot + 1)
                    pool.sem_inc(ids_passed, 1)
                    for f in range(NF):
                        nc.gpsimd.indirect_dma_start(
                            out=rows_e[:, slot, f * K:(f + 1) * K], out_offset=None, in_=tables[f],
                            in_offset=bass.IndirectOffsetOnAxis(ap=ids_now[:, slot, f:f + 1], axis=0),
                        ).then_inc(gathered[slot], 16)

        @block.vector
        def _(dve):
            for u in range(2):
                nc.vector.memset(block_e[:, u], 0.0).then_inc(zeroed, 1)
                nc.vector.memset(pairs[:, u, :, :, NP:NP + 1], 1.0).then_inc(slot_free, 1)

            dve.wait_ge(w1_in, 16)
            dve.wait_ge(b_in, 32)
            nc.vector.tensor_copy(view(w1_sym, NP, [1, 1]), bias_in[:, 0:1]).then_inc(w1_sym_ready, 1)
            nc.vector.tensor_tensor(view(w1_sym, AB, [GF, GF], [1, GF]), view(w1_raw, GF, [NF, GF], [1, GF]),
                                    view(w1_raw, GF * NF, [1, GF], [NF, GF]), ALU.add).then_inc(w1_sym_ready, 1)
            for g in range(2):
                at, f0 = (0, 0) if g == 0 else (NP + 1, GF)
                nc.vector.tensor_copy(view(w1_sym, at, [1, GF]),
                                      view(w1_raw, f0 * (NF + 1), [NF + 1, GF])).then_inc(w1_sym_ready, 1)
                for d in range(1, ND):
                    for i, n, back in rotations(d):
                        a, b = f0 + i, f0 + i + d - back
                        nc.vector.tensor_tensor(view(w1_sym, at + d * GF + i, [1, n]),
                                                view(w1_raw, a * NF + b, [NF + 1, n]),
                                                view(w1_raw, b * NF + a, [NF + 1, n]), ALU.add).then_inc(w1_sym_ready, 1)
            nc.vector.tensor_copy(view(gram_w_rows, 0, [GF, GF], [1, GF]),
                                  view(w1_raw, 0, [1, GF], [NF, GF])).then_inc(gram_rows_ready, 1)
            nc.vector.tensor_tensor(view(gram_w_rows, GF * GF, [GF, GF], [1, GF]), view(w1_raw, GF, [1, GF], [NF, GF]),
                                    view(w1_raw, GF * NF, [NF, GF], [1, GF]), ALU.add).then_inc(gram_rows_ready, 1)
            nc.vector.tensor_copy(view(gram_w_rows, NF * GF, [GF, GF], [1, GF]),
                                  view(w1_raw, GF * NF + GF, [1, GF], [NF, GF])).then_inc(gram_rows_ready, 1)
            nc.vector.tensor_scalar(bias_z[:], bias_in[:], float(K), None, ALU.mult).then_inc(bias_ready, 1)

            dve.wait_ge(ring_drained, first_cin + NF)
            steps = 0
            for term in range(2):
                for g in range(2):
                    l0, at, f0 = (GF, 0, 0) if g == 0 else (0, NP + 1, GF)
                    xs, ls = (GF, 1) if g == 0 else (1, GF)
                    for d in range(ND):
                        if term == 1 and d == 0:
                            continue
                        for i, n, back in rotations(d):
                            j = i + d - back
                            last, kept = (j, i) if term == 0 else (i, j)
                            dst = view(cin_w, l0 * RW + at + d * GF + i, [RW, GF], [1, n])
                            src = view(cin_w, (f0 + last) * RW + AB + kept * xs, [ls, GF], [RW + xs, n])
                            nc.vector.tensor_tensor(dst, dst, src, ALU.add).then_inc(
                                sym_step if term == 0 else cin_w_ready, 1)
                            steps += term == 0
                if term == 0:
                    dve.wait_ge(sym_step, steps)

            dve.wait_ge(zeroed, 2)
            with dve.Fori(0, HALVES) as half:
                for tile in range(TILES):
                    slot = tile % 2
                    dve.wait_ge(gathered[slot], half * (16 * NF * TILES // 2) + 16 * NF * (tile // 2 + 1))
                    dve.wait_ge(unit_ready, half * (TILES * 2 * UNIT_OPS) + tile * (2 * UNIT_OPS))
                    for g in range(2):
                        for dst, n in ((g * FX, GF), (g * FX + GF, ND - 1)):
                            ins = nc.vector.transpose(view(emb_t[:], dst * BT, [1, n * BT]),
                                                      rows_e[:, slot, g * GF * K:(g * GF + n) * K])
                            ins.then_inc(emb_ready if dst + n < 2 * FX else slot_free, 1)
                    dve.wait_ge(emb_ready, half * (TILES * 3) + tile * 3 + 3)
                    dve.wait_ge(slot_free, half * TILES + tile + 3)
                    for u in range(2):
                        v = tile * 2 + u
                        dve.wait_ge(unit_free, half * (TILES * 2 + 1) + (v if v >= 2 else 0))
                        b0 = u * UB
                        pb = pairs[:, u].rearrange("p b g r -> p (b g r)")
                        for g in range(2):
                            nc.vector.tensor_tensor(
                                view(pb, g * R, [2 * R, UB], [GF, ND], [1, GF]),
                                view(emb_t[:], g * FX * BT + b0, [1, UB], [0, ND], [BT, GF]),
                                view(emb_t[:], g * FX * BT + b0, [1, UB], [BT, ND], [BT, GF]),
                                ALU.mult).then_inc(unit_ready, 1)
                        nc.vector.tensor_copy(view(pb, NP + 1, [2 * R, UB], [R, 2], [1, GF]),
                                              view(emb_t[:], b0, [1, UB], [FX * BT, 2], [BT, GF])).then_inc(unit_ready, 1)
                        for q in range(Q):
                            part = slice(q * K, (q + 1) * K)
                            ins = nc.vector.tensor_copy(
                                view(block_e[part, u].rearrange("p b q f -> p (b q f)"), q * NF, [Q * NF, UB], [GF, 2], [1, GF]),
                                view(emb_t[part], b0, [1, UB], [FX * BT, 2], [BT, GF]))
                            ins.then_inc(unit_ready, 1)

        @block.tensor
        def _(pe):
            fill = [0]

            def ring_bank():
                n = fill[0]
                fill[0] += 1
                if n >= 4:
                    pe.wait_ge(ring_drained, n - 3)
                return ring[n % 4]

            pe.wait_ge(ident_ready, 1)
            pe.wait_ge(w2_in, 16)
            w2v = w2_raw.rearrange("h (i l) -> h i l", l=NF)
            for c in range(n_w2t):
                bank = ring_bank()
                fs = range(4 * c, min(4 * c + 4, NF))
                for f in fs:
                    mm = nc.tensor.transpose(bank[:, (f % 4) * H:(f % 4 + 1) * H], w2v[:, :, f], ident[:])
                mm.then_inc(ring_full, 1)
            pe.wait_ge(gram_rows_ready, 3)
            bank = ring_bank()
            for c in range(NG):
                n = min(GC, GRAMS - c * GC)
                mm = nc.tensor.transpose(bank[0:n, c * H:(c + 1) * H], gram_w_rows[:, c * GC:c * GC + n], ident[:])
            mm.then_inc(ring_full, 1)
            pe.wait_ge(dense_in, 16)
            for c in range(n_dense):
                bank = ring_bank()
                for t in range(TILES):
                    mm = nc.tensor.transpose(bank[0:DC, t * P:(t + 1) * P], dense_rows[:, c * TILES + t, :], ident[:])
                mm.then_inc(ring_full, 1)
            pe.wait_ge(w1_sym_ready, 4 + 4 * (ND - 1))
            for f in range(NF):
                bank = ring_bank()
                nc.tensor.matmul(bank[:, 0:RW], w2_t[:, f * H:(f + 1) * H], w1_sym,
                                 start=True, stop=True).then_inc(ring_full, 1)
            n_sym = 2 * 2 * (ND - 1)
            pe.wait_ge(cin_w_ready, n_sym)
            for c in range(n_v):
                bank = ring_bank()
                for v in range(4 * c, 4 * c + 4):
                    g, f = v // NF, v % NF
                    at = f * RW + g * (NP + 1)
                    mm = nc.tensor.transpose(bank[0:NP + 1, (v % 4) * H:(v % 4 + 1) * H],
                                             cin_w[:, at:at + NP + 1], ident[:])
                mm.then_inc(ring_full, 1)

            pe.wait_ge(mlp_w_in, 16 * 6)
            with pe.Fori(0, HALVES) as half:
                with pe.Fori(0, TILES) as tile:
                    for u in range(2):
                        pe.wait_ge(unit_ready, half * (TILES * 2 * UNIT_OPS) + tile * (2 * UNIT_OPS) + (u + 1) * UNIT_OPS)
                        for quad in range(UB // QUAD):
                            for g in range(2):
                                n = first_main + (u * (UB // QUAD) + quad) * 2 + g
                                bank = ring[n % 4]
                                pe.wait_ge(ring_drained, half * FILLS_H + tile * (FILLS_T // TILES) + n - 3)
                                for b in range(quad * QUAD, (quad + 1) * QUAD):
                                    mm = nc.tensor.matmul(bank[0:R, b % QUAD * Q * NF:(b % QUAD + 1) * Q * NF],
                                                          pairs[:, u, b, g, :],
                                                          block_e[:, u, b].rearrange("p q f -> p (q f)"),
                                                          start=True, stop=True)
                                    if quad == g == b == 0:
                                        mm.then_inc(unit_free, 1)
                                mm.then_inc(ring_full, 1)
                pe.wait_ge(ring_drained, half * FILLS_H + first_main + FILLS_T)
                pe.wait_ge(y_ready, half)
                for v in range(2 * NF):
                    rows = NP + 1 if v < NF else NP
                    mm = nc.tensor.matmul(z_bank[1][:, :], cubic_w[0:rows, v, :], moments[0:rows, v * HB:(v + 1) * HB],
                                          start=(v == 0), stop=(v == 2 * NF - 1))
                    if v == 0:
                        mm.then_inc(unit_free, 1)
                mm.then_inc(z_full, 1)
                pe.wait_ge(gram_in, half * (16 * GRAM_DMAS) + 16 * GRAM_DMAS)
                for c in range(NG):
                    rows = min(GC, GRAMS - c * GC)
                    mm = nc.tensor.matmul(z_bank[0][:, :], gram_w[0:rows, c, :], gram[0:rows, c, :],
                                          start=(c == 0), stop=(c == NG - 1))
                mm.then_inc(z_full, 1)
                pe.wait_ge(z_ready, half * 2 + 2)
                for m in range(C1):
                    n = first_main + FILLS_T + m
                    bank = ring[n % 4]
                    pe.wait_ge(ring_drained, half * FILLS_H + n - 3)
                    cols = slice(m * P, (m + 1) * P)
                    for c in range(2):
                        nc.tensor.matmul(bank[:, :], wt1[:, c, cols], z_sb[:, c * HB:(c + 1) * HB], start=(c == 0), stop=False)
                    nc.tensor.matmul(bank[:, :], wt1[0:DC, 2, cols], dense_t[:, bass.ds(half * HB, HB)],
                                     start=False, stop=True).then_inc(ring_full, 1)
                for m in range(C2):
                    for c in range(C1):
                        if m == 0:
                            pe.wait_ge(ring_drained, half * FILLS_H + first_main + FILLS_T + c + 1)
                        mm = nc.tensor.matmul(h2_bank[m][:, :], wt2[:, c, m * P:(m + 1) * P], h1_sb[:, c * HB:(c + 1) * HB],
                                              start=(c == 0), stop=(c == C1 - 1))
                    mm.then_inc(h2_full, 1)
                for c in range(C2):
                    pe.wait_ge(h2_ready, half * C2 + c + 1)
                    mm = nc.tensor.matmul(z_bank[1][0:1, :], wt3[:, c:c + 1], h2_sb[:, c * HB:(c + 1) * HB],
                                          start=(c == 0), stop=(c == C2 - 1))
                mm.then_inc(y_full, 1)

        @block.scalar
        def _(act):
            def drain(n, dst, rows, cols):
                act.wait_ge(ring_full, n + 1)
                nc.scalar.activation(dst, ring[n % 4][0:rows, 0:cols], ACT.Copy).then_inc(ring_drained, 1)

            n = 0
            for c in range(n_w2t):
                w = min(4, NF - 4 * c) * H
                drain(n, w2_t[:, 4 * c * H:4 * c * H + w], P, w)
                n += 1
            act.wait_ge(ring_full, n + 1)
            nc.scalar.activation(gram_w[0:GC, 0:NG - 1, :], ring[n % 4][0:GC, 0:(NG - 1) * H].rearrange(
                "p (c h) -> p c h", h=H), ACT.Copy)
            nc.scalar.activation(gram_w[0:G_LAST, NG - 1, :], ring[n % 4][0:G_LAST, (NG - 1) * H:NG * H],
                                 ACT.Copy).then_inc(ring_drained, 1)
            n += 1
            for c in range(n_dense):
                drain(n, dense_t[:, c * HB:(c + 1) * HB], DC, HB)
                n += 1
            for f in range(NF):
                drain(n, cin_w[:, f * RW:(f + 1) * RW], P, RW)
                n += 1
            cw = cubic_w[:].rearrange("p v h -> p (v h)")
            for c in range(n_v):
                drain(n, cw[:, 4 * c * H:(4 * c + 4) * H], NP + 1, 4 * H)
                n += 1

            act.wait_ge(bias_ready, 1)
            act.wait_ge(mlp_w_in, 16 * 6)
            with act.Fori(0, HALVES) as half:
                act.wait_ge(y_out, half * 16)
                with act.Fori(0, TILES) as tile:
                    for u in range(2):
                        for quad in range(UB // QUAD):
                            for g in range(2):
                                n = first_main + (u * (UB // QUAD) + quad) * 2 + g
                                act.wait_ge(ring_full, half * FILLS_H + tile * (FILLS_T // TILES) + n + 1)
                                dst = moments[0:R, bass.ds(tile * P + (g * NF * HB + u * UB + quad * QUAD), HB * (NF - 1) + P - BT + QUAD)]
                                dst = view(dst, 0, [BT, Q], [HB, NF], [1, QUAD])
                                src = view(ring[n % 4][0:R, :], 0, [NF, Q], [1, NF], [Q * NF, QUAD])
                                nc.scalar.activation(dst, src, ACT.Copy).then_inc(ring_drained, 1)
                act.wait_ge(z_full, half * 2 + 2)
                for c, bank in ((1, z_bank[1]), (0, z_bank[0])):
                    nc.scalar.activation(z_sb[:, c * HB:(c + 1) * HB], bank[:, :], ACT.Identity,
                                         bias=bias_z[:, c:c + 1]).then_inc(z_ready, 1)
                for m in range(C1):
                    n = first_main + FILLS_T + m
                    act.wait_ge(ring_full, half * FILLS_H + n + 1)
                    nc.scalar.activation(h1_sb[:, m * HB:(m + 1) * HB], ring[n % 4][:, :], ACT.Relu,
                                         bias=bias1[:, m:m + 1]).then_inc(ring_drained, 1)
                for m in range(C2):
                    act.wait_ge(h2_full, half * C2 + m + 1)
                    nc.scalar.activation(h2_sb[:, m * HB:(m + 1) * HB], h2_bank[m][:, :], ACT.Relu,
                                         bias=bias2[:, m:m + 1]).then_inc(h2_ready, 1)
                act.wait_ge(y_full, half + 1)
                nc.scalar.activation(y_row, z_bank[1][0:1, :], ACT.Copy).then_inc(y_ready, 1)


_TABLES = [f"tbl_{f}" for f in range(26)]
_INS = ["dense_ctx", "ids"] + _TABLES + ["W_top1", "b_top1", "W_top2", "b_top2", "W_top3",
                                         "L0_rec_W1", "L0_rec_b1", "L0_rec_W2", "L0_rec_b2"]


def kernel(**inputs):
    import numpy as _np
    import concourse.bacc as _bacc
    from concourse import mybir as _mybir
    from concourse.bass_utils import run_bass_kernel_spmd as _run

    nc = _bacc.Bacc("TRN2", target_bir_lowering=False, num_devices=1)
    arrays, aps = {}, {}
    for name in _INS:
        a = _np.ascontiguousarray(inputs[name])
        arrays[f"in_{name}_dram"] = a
        aps[name] = nc.dram_tensor(f"in_{name}_dram", a.shape, _mybir.dt.from_np(a.dtype), kind="ExternalInput").ap()
    out = nc.dram_tensor("out_0_dram", (inputs["dense_ctx"].shape[0], 1), _mybir.dt.float32, kind="ExternalOutput").ap()
    build_tower(nc, aps["dense_ctx"], aps["ids"], [aps[t] for t in _TABLES], aps["W_top1"], aps["b_top1"],
                aps["W_top2"], aps["b_top2"], aps["W_top3"], aps["L0_rec_W1"], aps["L0_rec_b1"],
                aps["L0_rec_W2"], aps["L0_rec_b2"], out)
    r = _run(nc, [arrays], core_ids=[0])
    return r.results[0]["out_0_dram"]
```

```python
from contextlib import ExitStack

import concourse.bass as bass
from concourse import mybir

F32 = mybir.dt.float32
I32 = mybir.dt.int32
ALU = mybir.AluOpType
ACT = mybir.ActivationFunctionType


def build_tower(nc, dense, ids, tables, w_top1, b_top1, w_top2, b_top2, w_top3, w1, b1, w2, b2, out, gram_rows):
    B, DC = dense.shape
    NF = len(tables)
    K = tables[0].shape[1]
    H = w1.shape[0]
    N1, N2 = w_top1.shape[1], w_top2.shape[1]
    P = 128
    Q = P // K
    NA, NU, NT = 13, 8, 5
    NB = NU + NT
    U0, T0 = NA, NA + NU

    def n_pairs(n):
        return n * (n + 1) // 2

    PA, PB, PT = n_pairs(NA), n_pairs(NB), n_pairs(NT)
    ONE_ROW = PA
    T_ROW = PA + 1
    CUBIC_ROWS = T_ROW + PT
    ROWS = (PB, CUBIC_ROWS + NA)
    L0, L1 = 1 + NA + NU, NF
    COLS = L0 + L1
    WRAP_A, WRAP_T = NA // 2, NT // 2
    SLOT_B = NA + WRAP_A
    SLOT_T = SLOT_B + NB + NU
    SLOTS = SLOT_B + 2 * NB + WRAP_T
    SLOT_L = WRAP_A
    l_order = [(WRAP_A + i) % NA for i in range(NA)] + list(range(NA, NF))
    C_BB = 0
    C_AA = C_BB + PB
    C_B1 = C_AA + PA
    C_TT = C_B1 + 1
    C_AB = C_TT + PT
    C_TU = C_AB + NA * NB
    C_UU = C_TU + NT * NU
    RW = C_UU + NU * NU
    UB = 16
    UNITS = 4
    BT = P // Q
    HB = 256
    BLOCKS = B // HB - 1
    QUAD = 4
    GRAMS = NA * NF
    NG = -(-GRAMS // P)
    GC = -(-GRAMS // NG)
    VR = max(PB, CUBIC_ROWS)
    C1, C2 = N1 // P, N2 // P
    FILLS_T = BT // QUAD * 2
    VOFF = [(0, l_order[i]) for i in range(NA + NU)] + [(1, f) for f in l_order]
    NV = len(VOFF)
    assert K == 32 and NF == NA + NB and NA % 2 and NB % 2 and NT % 2 and H == P
    assert RW <= 512 and COLS == NV + 1 and NG == 3 and NA == NB and C_AA + VR <= RW

    with ExitStack() as ctx:
        def sb(name, shape, dt=F32):
            return ctx.enter_context(nc.sbuf_tensor(name, shape, dt))

        def sem(name):
            return ctx.enter_context(nc.semaphore(name))

        moments = sb("moments", [P, COLS * HB])
        cubic_w = sb("cubic_w", [VR, NV, H])
        pairs = sb("pairs", [P, UNITS, UB, sum(ROWS)])
        block_e = sb("block_e", [P, UNITS, UB, Q, 1 + NF])
        rows_e = sb("rows_e", [P, 2, NF * K])
        emb_t = sb("emb_t", [P, SLOTS, BT])
        late = sb("late", [P, NB * RW])
        gram_w = sb("gram_w", [GC, NG + 1, H])
        wt1 = sb("wt1", [P, 3, N1])
        wt2 = sb("wt2", [P, C1, N2])
        wt3 = sb("wt3", [P, C2])
        dense_y = sb("dense_y", [P, B])
        dense_t = dense_y[0:DC, :]
        y_all = dense_y[32:33, :]
        ids_all = sb("ids_all", [P, B // P, NF], I32)
        ids_now = sb("ids_now", [P, 2, NF], I32)
        ident = sb("ident", [P, P])
        bias1 = sb("bias1", [P, C1])
        bias2 = sb("bias2", [P, C2])
        bias_in = sb("bias_in", [P, 2])
        bias_z = sb("bias_z", [P, 2])

        ring = [ctx.enter_context(nc.psum_tensor(f"ring{i}", [P, 512], F32)) for i in range(4)]
        z_bank = [ctx.enter_context(nc.psum_tensor(f"z_bank{i}", [P, 512], F32)) for i in range(2)]
        h2_bank = [ctx.enter_context(nc.psum_tensor(f"h2_bank{i}", [P, 512], F32)) for i in range(2)]

        class Region:

            def __init__(self, base):
                self.base, self.at = base, 0

            def take(self, n):
                self.at += n
                return self.base[:, self.at - n:self.at]

            def take3(self, c, n):
                return self.take(c * n).rearrange("p (c n) -> p c n", n=n)

        pre = Region(moments)
        w1_raw = pre.take(NF * NF)
        w2_raw = pre.take(H * NF)
        w2_t = pre.take(NF * H)
        w1_sym = pre.take(RW)
        gram_w_rows = pre.take(GRAMS)
        dense_rows = pre.take3(B // P, DC)
        cin_a = pairs[:, 2:4].rearrange("p u b r -> p (u b r)")[:, 0:NA * RW]
        cin_b = late[:, 0:NB * RW]
        layers = Region(late)
        gram = layers.take3(NG, HB)
        z_sb = layers.take3(2, HB)
        h1_sb = layers.take3(C1, HB)
        h2_sb = layers.take3(C2, HB)

        def cin(f):
            return (cin_a, f * RW) if f < NA else (cin_b, (f - NA) * RW)

        pairs_flat = [pairs[:, u].rearrange("p b r -> p (b r)") for u in range(UNITS)]
        block_flat = [block_e[:, u].rearrange("p b q f -> p (b q f)") for u in range(UNITS)]
        RS = sum(ROWS)
        QS = 1 + NF
        emb = emb_t[:].rearrange("p s b -> p (s b)")

        def view(base, off, *dims):
            return bass.AP(base.tensor, base.offset + off, [list(base.ap[0])] + [list(d) for d in dims])

        ids_in = sem("ids_in")
        w1_in, w2_in, b_in, dense_in = sem("w1_in"), sem("w2_in"), sem("b_in"), sem("dense_in")
        mlp_w_in = sem("mlp_w_in")
        gathered = [sem("gathered0"), sem("gathered1")]
        gram_out, gram_in = sem("gram_out"), sem("gram_in")
        y_out = sem("y_out")
        ident0, ident_ready, ids_copied = sem("ident0"), sem("ident_ready"), sem("ids_copied")
        ids_passed = sem("ids_passed")
        slot_free = sem("slot_free")
        emb_ready = sem("emb_ready")
        unit_ready = sem("unit_ready")
        w1_sym_ready, gram_rows_ready = sem("w1_sym_ready"), sem("gram_rows_ready")
        sym_step, cin_w_ready, bias_ready = sem("sym_step"), sem("cin_w_ready"), sem("bias_ready")
        begun = sem("begun")
        ring_full = sem("ring_full")
        z_full, h2_full, y_full = sem("z_full"), sem("h2_full"), sem("y_full")
        ring_drained = sem("ring_drained")
        z_ready, h2_ready, y_ready = sem("z_ready"), sem("h2_ready"), sem("y_ready")

        n_w2t = -(-NF // 4)
        n_dense = B // 512
        n_v = -(-NV // 4)
        first_gw = n_w2t
        first_dense = first_gw + 1
        first_cin = first_dense + n_dense
        first_main = first_cin + NF
        first_v = first_main + FILLS_T
        FILLS_B = 2 * FILLS_T + C1
        assert FILLS_B % 4 == 0 and (FILLS_T + C1) % 4 == 0 and n_v % 4 == 0
        CONSTS0 = UNITS + UNITS * Q + 2
        CONSTS = CONSTS0 + 2
        UNIT_OPS = 4 + Q

        def full_block(i, before_v=False):
            return dict(fills=i * FILLS_B + (0 if before_v else n_v), units=i * 4, blocks=i, tile=i * 2, tiles=2)

        def tile_block(i):
            return dict(fills=BLOCKS * FILLS_B + n_v + i * (FILLS_T + C1), units=BLOCKS * 4 + i * 2, blocks=BLOCKS + i,
                        tile=BLOCKS * 2 + i, tiles=1)

        def dense_at(at, w):
            return slice(at, at + w) if isinstance(at, int) else bass.ds(at, w)

        N_SYM = sum(1 + 2 * (n // 2) for n in (NA, NB, NT)) + 4
        N_FIRST = sum(1 + 2 * (n // 2) for n in (NA, NB)) + NT + NB - 1
        N_SECOND = sum(2 * (n // 2) for n in (NA, NB)) + NT - 1

        def rotations(n, d):
            return [(0, n, 0)] if d == 0 else [(0, n - d, 0), (n - d, d, n)]

        block = ctx.enter_context(nc.Block())

        @block.sync
        def _(sp):
            sp.dma_start(ids_all[:], ids.rearrange("(t p) f -> p t f", p=P)).then_inc(ids_in, 16)
            sp.dma_start(w2_raw, w2.rearrange("h i l -> h (i l)")).then_inc(w2_in, 16)
            sp.dma_start(w1_raw, w1.rearrange("h i j -> h (i j)")).then_inc(w1_in, 16)
            sp.dma_start(bias_in[:, 0:1], b1.rearrange("(h a) -> h a", a=1)).then_inc(b_in, 16)
            sp.dma_start(bias_in[:, 1:2], b2.rearrange("(h a) -> h a", a=1)).then_inc(b_in, 16)
            sp.dma_start(dense_rows, dense.rearrange("(t p) c -> p t c", p=P)).then_inc(dense_in, 16)
            sp.dma_start(wt1[:, 0:2, :], w_top1[0:2 * P, :].rearrange("(c p) n -> p c n", p=P)).then_inc(mlp_w_in, 16)
            sp.dma_start(wt1[0:DC, 2, :], w_top1[2 * P:2 * P + DC, :]).then_inc(mlp_w_in, 16)
            sp.dma_start(wt2[:], w_top2.rearrange("(c p) n -> p c n", p=P)).then_inc(mlp_w_in, 16)
            with nc.allow_non_contiguous_dma(reason="small vectors onto the partitions"):
                sp.dma_start(wt3[:], w_top3.rearrange("(c p) a -> p (c a)", p=P)).then_inc(mlp_w_in, 16)
                sp.dma_start(bias1[:], b_top1.rearrange("(c p) -> p c", p=P)).then_inc(mlp_w_in, 16)
                sp.dma_start(bias2[:], b_top2.rearrange("(c p) -> p c", p=P)).then_inc(mlp_w_in, 16)

            def stack_gram(k):
                w = k["tiles"] * P
                sp.wait_ge(ring_drained, k["fills"] + first_main + k["tiles"] * FILLS_T)
                src = view(moments[CUBIC_ROWS:ROWS[1]], L0 * HB, [HB, NF], [1, w])
                sp.dma_start(gram_rows[:, :, 0:w], src).then_inc(gram_out, 16)
                sp.wait_ge(gram_out, k["blocks"] * 16 + 16)
                rows = gram_rows.rearrange("i l b -> (i l) b")
                for c in range(NG):
                    n = min(GC, GRAMS - c * GC)
                    sp.dma_start(gram[0:n, c, 0:w], rows[c * GC:c * GC + n, 0:w]).then_inc(gram_in, 16)

            with sp.Fori(0, BLOCKS) as i:
                stack_gram(full_block(i))
            for i in range(2):
                stack_gram(tile_block(i))
            sp.wait_ge(y_ready, BLOCKS + 2)
            sp.dma_start(out.rearrange("b a -> a b"), y_all).then_inc(y_out, 16)
            sp.wait_ge(y_out, 16)

        @block.gpsimd
        def _(pool):
            nc.gpsimd.memset(ident[:], 0.0).then_inc(ident0, 1)
            pool.wait_ge(ident0, 1)
            nc.gpsimd.affine_select(out=ident[:], in_=ident[:], pattern=[[-1, P]], compare_op=ALU.not_equal,
                                    fill=1.0, base=0, channel_multiplier=1).then_inc(ident_ready, 1)
            pool.sem_inc(slot_free, 2)
            pool.wait_ge(ids_in, 16)
            with pool.Fori(0, B // P // 2) as pair:
                for slot in range(2):
                    pool.wait_ge(slot_free, pair * 2 + slot + 1)
                    nc.gpsimd.tensor_copy(ids_now[:, slot, :], ids_all[:, bass.ds(pair * 2 + slot, 1), :]).then_inc(ids_copied, 1)
                    pool.wait_ge(ids_copied, pair * 2 + slot + 1)
                    pool.sem_inc(ids_passed, 1)
                    for f in range(NF):
                        nc.gpsimd.indirect_dma_start(
                            out=rows_e[:, slot, f * K:(f + 1) * K], out_offset=None, in_=tables[f],
                            in_offset=bass.IndirectOffsetOnAxis(ap=ids_now[:, slot, f:f + 1], axis=0),
                        ).then_inc(gathered[slot], 16)

        @block.vector
        def _(dve):
            def add(dst, a, b, signal):
                nc.vector.tensor_tensor(dst, a, b, ALU.add).then_inc(signal, 1)

            def copy(dst, src, signal):
                nc.vector.tensor_copy(dst, src).then_inc(signal, 1)

            def ones_row(u):
                nc.vector.memset(pairs[:, u, :, PB + ONE_ROW:PB + ONE_ROW + 1], 1.0).then_inc(unit_ready, 1)

            for u in range(UNITS):
                nc.vector.memset(block_e[:, u], 0.0).then_inc(unit_ready, 1)
            dve.wait_ge(unit_ready, UNITS)
            for u in range(UNITS):
                for q in range(Q):
                    nc.vector.memset(block_e[q * K:(q + 1) * K, u, :, q, 0:1], 1.0).then_inc(unit_ready, 1)
            for u in range(2):
                ones_row(u)

            dve.wait_ge(w1_in, 16)
            dve.wait_ge(b_in, 32)
            for at, n, f0 in ((C_BB, NB, U0), (C_AA, NA, 0), (C_TT, NT, T0)):
                copy(view(w1_sym, at, [1, n]), view(w1_raw, f0 * (NF + 1), [NF + 1, n]), w1_sym_ready)
                for d in range(1, n // 2 + 1):
                    for i, m, wrap in rotations(n, d):
                        a, b = f0 + i, f0 + i + d - wrap
                        add(view(w1_sym, at + d * n + i, [1, m]), view(w1_raw, a * NF + b, [NF + 1, m]),
                            view(w1_raw, b * NF + a, [NF + 1, m]), w1_sym_ready)
            copy(view(w1_sym, C_B1, [1, 1]), bias_in[:, 0:1], w1_sym_ready)
            add(view(w1_sym, C_AB, [NB, NA], [1, NB]), view(w1_raw, U0, [NF, NA], [1, NB]),
                view(w1_raw, U0 * NF, [1, NA], [NF, NB]), w1_sym_ready)
            add(view(w1_sym, C_TU, [NU, NT], [1, NU]), view(w1_raw, T0 * NF + U0, [NF, NT], [1, NU]),
                view(w1_raw, U0 * NF + T0, [1, NT], [NF, NU]), w1_sym_ready)
            copy(view(w1_sym, C_UU, [NU, NU], [1, NU]), view(w1_raw, U0 * NF + U0, [NF, NU], [1, NU]), w1_sym_ready)
            first = NA - WRAP_A
            copy(view(gram_w_rows, 0, [NF, NA], [1, first]), view(w1_raw, WRAP_A, [NF, NA], [1, first]), gram_rows_ready)
            copy(view(gram_w_rows, first, [NF, NA], [1, WRAP_A]), view(w1_raw, 0, [NF, NA], [1, WRAP_A]), gram_rows_ready)
            add(view(gram_w_rows, NA, [NF, NA], [1, NB]), view(w1_raw, U0, [NF, NA], [1, NB]),
                view(w1_raw, U0 * NF, [1, NA], [NF, NB]), gram_rows_ready)
            nc.vector.tensor_scalar(bias_z[:], bias_in[:], float(K), None, ALU.mult).then_inc(bias_ready, 1)

            def fold(dst, src, signal):
                add(dst, dst, src, signal)

            def cin_view(f, column, *dims):
                part, at = cin(f)
                return view(part, at + column, *dims)

            def first_pass(sig):
                for n, at, own0, l0, nl, ls, xs in ((NA, C_AA, 0, U0, NB, 1, NB), (NB, C_BB, U0, 0, NA, NB, 1)):
                    for d in range(n // 2 + 1):
                        for i, m, wrap in rotations(n, d):
                            j = i + d - wrap
                            fold(cin_view(l0, at + d * n + i, [RW, nl], [1, m]),
                                 cin_view(own0 + j, C_AB + i * xs, [ls, nl], [RW + xs, m]), sig)
                for d in range(NT):
                    fold(tu_cell(d), cin_view(T0 + d, C_TU, [1, NU], [RW + NU, NT - d]), sig)
                for e in range(1, NB):
                    u_lo, u_hi = max(0, NU - e), min(NU - 1, NB - 1 - e)
                    at = e * NB + u_lo if e <= NB // 2 else (NB - e) * NB + e + u_lo
                    m = u_hi - u_lo + 1
                    fold(cin_view(U0, C_BB + at, [RW, NU], [1, m]),
                         cin_view(U0 + e + u_lo, C_UU + u_lo, [NU, NU], [RW + 1, m]), sig)

            def tu_cell(d):
                at = d * NB + NU if d <= NB // 2 else (NB - d) * NB + NU + d
                return cin_view(U0, C_BB + at, [RW, NU], [1, NT - d])

            def second_pass(sig):
                for n, at, own0, l0, nl, ls, xs in ((NA, C_AA, 0, U0, NB, 1, NB), (NB, C_BB, U0, 0, NA, NB, 1)):
                    for d in range(1, n // 2 + 1):
                        for i, m, wrap in rotations(n, d):
                            j = i + d - wrap
                            fold(cin_view(l0, at + d * n + i, [RW, nl], [1, m]),
                                 cin_view(own0 + i, C_AB + j * xs, [ls, nl], [RW + xs, m]), sig)
                for d in range(1, NT):
                    fold(tu_cell(d), cin_view(T0, C_TU + d * NU, [1, NU], [RW + NU, NT - d]), sig)

            def tile_units(slot, gathers, made, tiles):
                dve.wait_ge(gathered[slot], gathers)
                dve.wait_ge(unit_ready, made)
                for dst, f, n, signal in ((0, 0, NA, emb_ready), (NA, 0, WRAP_A, emb_ready), (SLOT_B, U0, NB, emb_ready),
                                          (SLOT_B + NB, U0, NB, emb_ready), (SLOT_B + 2 * NB, T0, WRAP_T, slot_free)):
                    nc.vector.transpose(view(emb, dst * BT, [1, n * BT]),
                                        rows_e[:, slot, f * K:(f + n) * K]).then_inc(signal, 1)
                dve.wait_ge(emb_ready, tiles * 4 + 4)
                dve.wait_ge(slot_free, tiles + 3)

            def make_unit(u, h):
                b0 = h * UB
                pb, be = pairs_flat[u], block_flat[u]
                for at, n, s in ((0, NB, SLOT_B), (PB, NA, 0), (PB + T_ROW, NT, SLOT_T)):
                    nc.vector.tensor_tensor(
                        view(pb, at, [RS, UB], [n, n // 2 + 1], [1, n]),
                        view(emb, s * BT + b0, [1, UB], [0, n // 2 + 1], [BT, n]),
                        view(emb, s * BT + b0, [1, UB], [BT, n // 2 + 1], [BT, n]),
                        ALU.mult).then_inc(unit_ready, 1)
                copy(view(pb, PB + CUBIC_ROWS, [RS, UB], [1, NA]), view(emb, b0, [1, UB], [BT, NA]), unit_ready)
                for q in range(Q):
                    part = slice(q * K, (q + 1) * K)
                    copy(view(be[part], q * QS + 1, [Q * QS, UB], [1, NF]),
                         view(emb[part], SLOT_L * BT + b0, [1, UB], [BT, NF]), unit_ready)

            tile_units(0, 16 * NF, CONSTS0, 0)
            for h in range(2):
                make_unit(h, h)

            dve.wait_ge(ring_drained, first_cin + NF)
            first_pass(sym_step)
            dve.wait_ge(sym_step, N_FIRST)
            second_pass(cin_w_ready)
            dve.wait_ge(ring_drained, first_v + n_v)
            for u in range(2, UNITS):
                ones_row(u)
            tile_units(1, 16 * NF, CONSTS + 2 * UNIT_OPS, 1)
            for h in range(2):
                make_unit(2 + h, h)

            with dve.Fori(1, B // P // 2) as pair:
                for slot in range(2):
                    tile_units(slot, pair * (16 * NF) + 16 * NF, pair * (4 * UNIT_OPS) + CONSTS + slot * 2 * UNIT_OPS,
                               pair * 2 + slot)
                    for h in range(2):
                        u = slot * 2 + h
                        dve.wait_ge(begun, pair * 5 + u + 1)
                        make_unit(u, h)

        @block.tensor
        def _(pe):
            fill = [0]

            def ring_bank():
                n = fill[0]
                fill[0] += 1
                if n >= 4:
                    pe.wait_ge(ring_drained, n - 3)
                return ring[n % 4]

            pe.wait_ge(ident_ready, 1)
            pe.wait_ge(w2_in, 16)
            w2v = w2_raw.rearrange("h (i l) -> h i l", l=NF)
            for c in range(n_w2t):
                bank = ring_bank()
                for f in range(4 * c, min(4 * c + 4, NF)):
                    mm = nc.tensor.transpose(bank[:, (f % 4) * H:(f % 4 + 1) * H], w2v[:, :, f], ident[:])
                    if f % 4 == 0 and c < UNITS:
                        mm.then_inc(begun, 1)
                mm.then_inc(ring_full, 1)
            pe.wait_ge(gram_rows_ready, 3)
            pe.wait_ge(w1_sym_ready, N_SYM)
            bank = ring_bank()
            for c in range(NG):
                n = min(GC, GRAMS - c * GC)
                nc.tensor.transpose(bank[0:n, c * H:(c + 1) * H], gram_w_rows[:, c * GC:c * GC + n], ident[:])
            nc.tensor.transpose(bank[0:PB, NG * H:(NG + 1) * H], w1_sym[:, C_BB:C_BB + PB], ident[:]).then_inc(ring_full, 1)
            pe.wait_ge(dense_in, 16)
            for c in range(n_dense):
                bank = ring_bank()
                for t in range(4):
                    mm = nc.tensor.transpose(bank[0:DC, t * P:(t + 1) * P], dense_rows[:, c * 4 + t, :], ident[:])
                mm.then_inc(ring_full, 1)
            for f in range(NF):
                bank = ring_bank()
                nc.tensor.matmul(bank[:, 0:RW], w2_t[:, f * H:(f + 1) * H], w1_sym,
                                 start=True, stop=True).then_inc(ring_full, 1)
            def transpose_cubic():
                pe.wait_ge(cin_w_ready, N_SECOND)
                for c in range(n_v):
                    n = first_v + c
                    bank = ring[n % 4]
                    pe.wait_ge(ring_drained, n - 3)
                    for v in range(4 * c, min(4 * c + 4, NV)):
                        g, f = VOFF[v]
                        part, at = cin(f)
                        at += C_BB if g == 0 else C_AA
                        mm = nc.tensor.transpose(bank[0:VR, (v % 4) * H:(v % 4 + 1) * H], part[:, at:at + VR], ident[:])
                    mm.then_inc(ring_full, 1)

            def unit_moments(k, tile_n, u, h, consts=CONSTS):
                pe.wait_ge(unit_ready, k["units"] * UNIT_OPS + (tile_n * 2 + h + 1) * UNIT_OPS + consts)
                for quad in range(UB // QUAD):
                    for g in range(2):
                        n = first_main + tile_n * FILLS_T + h * (FILLS_T // 2) + quad * 2 + g
                        bank = ring[n % 4]
                        pe.wait_ge(ring_drained, k["fills"] + n - 3)
                        cols = L0 if g == 0 else L1
                        for b in range(quad * QUAD, (quad + 1) * QUAD):
                            at = b % QUAD * Q * cols
                            mm = nc.tensor.matmul(bank[0:ROWS[g], at:at + Q * cols],
                                                  pairs[:, u, b, 0:PB] if g == 0 else pairs[:, u, b, PB:RS],
                                                  view(block_flat[u], b * Q * QS + g, [QS, Q], [1, cols]),
                                                  start=True, stop=True)
                            if quad == g == b == 0:
                                mm.then_inc(begun, 1)
                        mm.then_inc(ring_full, 1)

            def block_layers(k):
                w = k["tiles"] * P
                moments_done = first_main + k["tiles"] * FILLS_T
                pe.wait_ge(ring_drained, k["fills"] + moments_done)
                for v in range(NV):
                    g, f = VOFF[v]
                    rows = PB if g == 0 else (CUBIC_ROWS if f >= T0 else T_ROW)
                    mm = nc.tensor.matmul(z_bank[1][:, 0:w], cubic_w[0:rows, v, :], moments[0:rows, (v + 1) * HB:(v + 1) * HB + w],
                                          start=(v == 0), stop=(v == NV - 1))
                    if v == 0:
                        mm.then_inc(begun, 1)
                mm.then_inc(z_full, 1)
                nc.tensor.matmul(z_bank[0][:, 0:w], gram_w[0:PB, NG, :], moments[0:PB, 0:w], start=True, stop=False)
                pe.wait_ge(gram_in, k["blocks"] * (16 * NG) + 16 * NG)
                for c in range(NG):
                    rows = min(GC, GRAMS - c * GC)
                    mm = nc.tensor.matmul(z_bank[0][:, 0:w], gram_w[0:rows, c, :], gram[0:rows, c, 0:w],
                                          start=False, stop=(c == NG - 1))
                mm.then_inc(z_full, 1)
                for part in range(3):
                    if part:
                        pe.wait_ge(z_ready, k["blocks"] * 2 + part)
                    for m in range(C1):
                        bank = ring[(moments_done + m) % 4]
                        cols = slice(m * P, (m + 1) * P)
                        if part == 0:
                            lhs, rhs = wt1[0:DC, 2, cols], dense_t[:, dense_at(k["tile"] * P, w)]
                        else:
                            lhs, rhs = wt1[:, 2 - part, cols], z_sb[:, 2 - part, 0:w]
                        mm = nc.tensor.matmul(bank[:, 0:w], lhs, rhs, start=(part == 0), stop=(part == 2))
                        if part == 2:
                            mm.then_inc(ring_full, 1)
                for c in range(C1):
                    pe.wait_ge(ring_drained, k["fills"] + moments_done + c + 1)
                    for m in range(C2):
                        mm = nc.tensor.matmul(h2_bank[m][:, 0:w], wt2[:, c, m * P:(m + 1) * P], h1_sb[:, c, 0:w],
                                              start=(c == 0), stop=(c == C1 - 1))
                        if c == C1 - 1:
                            mm.then_inc(h2_full, 1)
                for c in range(C2):
                    pe.wait_ge(h2_ready, k["blocks"] * C2 + c + 1)
                    mm = nc.tensor.matmul(z_bank[1][32:33, 0:w], wt3[:, c:c + 1], h2_sb[:, c, 0:w],
                                          start=(c == 0), stop=(c == C2 - 1))
                mm.then_inc(y_full, 1)

            pe.wait_ge(mlp_w_in, 16 * 6)
            k = full_block(0, before_v=True)
            for h in range(2):
                unit_moments(k, 0, h, h, CONSTS0)
            transpose_cubic()
            k = full_block(0)
            for h in range(2):
                unit_moments(k, 1, 2 + h, h)
            block_layers(k)
            with pe.Fori(1, BLOCKS) as i:
                k = full_block(i)
                for tile in range(2):
                    for h in range(2):
                        unit_moments(k, tile, tile * 2 + h, h)
                block_layers(k)
            for i in range(2):
                k = tile_block(i)
                for h in range(2):
                    unit_moments(k, 0, i * 2 + h, h)
                block_layers(k)

        @block.scalar
        def _(act):
            def drain(n, dst, rows, cols):
                act.wait_ge(ring_full, n + 1)
                nc.scalar.activation(dst, ring[n % 4][0:rows, 0:cols], ACT.Copy).then_inc(ring_drained, 1)

            n = 0
            for c in range(n_w2t):
                w = min(4, NF - 4 * c) * H
                drain(n, w2_t[:, 4 * c * H:4 * c * H + w], P, w)
                n += 1
            act.wait_ge(ring_full, n + 1)
            for c in range(NG):
                rows = min(GC, GRAMS - c * GC)
                nc.scalar.activation(gram_w[0:rows, c, :], ring[n % 4][0:rows, c * H:(c + 1) * H], ACT.Copy)
            nc.scalar.activation(gram_w[0:PB, NG, :], ring[n % 4][0:PB, NG * H:(NG + 1) * H], ACT.Copy).then_inc(ring_drained, 1)
            n += 1
            for c in range(n_dense):
                drain(n, dense_t[:, c * 512:(c + 1) * 512], DC, 512)
                n += 1
            for f in range(NF):
                part, at = cin(f)
                drain(n, part[:, at:at + RW], P, RW)
                n += 1
            def tile_moments(k, tile_n):
                for h in range(2):
                    for quad in range(UB // QUAD):
                        for g in range(2):
                            n = first_main + tile_n * FILLS_T + h * (FILLS_T // 2) + quad * 2 + g
                            cols, rows = (L0, L1)[g], ROWS[g]
                            act.wait_ge(ring_full, k["fills"] + n + 1)
                            dst = view(moments[0:rows], g * L0 * HB + tile_n * P + h * UB + quad * QUAD, [BT, Q], [HB, cols], [1, QUAD])
                            src = view(ring[n % 4][0:rows, :], 0, [cols, Q], [1, cols], [Q * cols, QUAD])
                            nc.scalar.activation(dst, src, ACT.Copy).then_inc(ring_drained, 1)

            def block_layers(k):
                w = k["tiles"] * P
                moments_done = first_main + k["tiles"] * FILLS_T
                for c in (1, 0):
                    act.wait_ge(z_full, k["blocks"] * 2 + 2 - c)
                    nc.scalar.activation(z_sb[:, c, 0:w], z_bank[c][:, 0:w], ACT.Identity,
                                         bias=bias_z[:, c:c + 1]).then_inc(z_ready, 1)
                for m in range(C1):
                    n = moments_done + m
                    act.wait_ge(ring_full, k["fills"] + n + 1)
                    nc.scalar.activation(h1_sb[:, m, 0:w], ring[n % 4][:, 0:w], ACT.Relu,
                                         bias=bias1[:, m:m + 1]).then_inc(ring_drained, 1)
                for m in range(C2):
                    act.wait_ge(h2_full, k["blocks"] * C2 + m + 1)
                    nc.scalar.activation(h2_sb[:, m, 0:w], h2_bank[m][:, 0:w], ACT.Relu,
                                         bias=bias2[:, m:m + 1]).then_inc(h2_ready, 1)
                act.wait_ge(y_full, k["blocks"] + 1)
                nc.scalar.activation(y_all[:, dense_at(k["tile"] * P, w)], z_bank[1][32:33, 0:w], ACT.Copy).then_inc(y_ready, 1)

            act.wait_ge(bias_ready, 1)
            act.wait_ge(mlp_w_in, 16 * 6)
            tile_moments(full_block(0, before_v=True), 0)
            cw = cubic_w[:].rearrange("p v h -> p (v h)")
            for c in range(n_v):
                w = min(4, NV - 4 * c) * H
                drain(first_v + c, cw[:, 4 * c * H:4 * c * H + w], VR, w)
            k = full_block(0)
            tile_moments(k, 1)
            block_layers(k)
            with act.Fori(1, BLOCKS) as i:
                k = full_block(i)
                for tile in range(2):
                    tile_moments(k, tile)
                block_layers(k)
            for i in range(2):
                k = tile_block(i)
                tile_moments(k, 0)
                block_layers(k)


_TABLES = [f"tbl_{f}" for f in range(26)]
_INS = ["dense_ctx", "ids"] + _TABLES + ["W_top1", "b_top1", "W_top2", "b_top2", "W_top3",
                                         "L0_rec_W1", "L0_rec_b1", "L0_rec_W2", "L0_rec_b2"]


def kernel(**inputs):
    import numpy as _np
    import concourse.bacc as _bacc
    from concourse import mybir as _mybir
    from concourse.bass_utils import run_bass_kernel_spmd as _run

    nc = _bacc.Bacc("TRN2", target_bir_lowering=False, num_devices=1)
    arrays, aps = {}, {}
    for name in _INS:
        a = _np.ascontiguousarray(inputs[name])
        arrays[f"in_{name}_dram"] = a
        aps[name] = nc.dram_tensor(f"in_{name}_dram", a.shape, _mybir.dt.from_np(a.dtype), kind="ExternalInput").ap()
    out = nc.dram_tensor("out_0_dram", (inputs["dense_ctx"].shape[0], 1), _mybir.dt.float32, kind="ExternalOutput").ap()
    gram_rows = nc.dram_tensor("gram_rows", (13, 26, 256), _mybir.dt.float32, kind="Internal").ap()
    build_tower(nc, aps["dense_ctx"], aps["ids"], [aps[t] for t in _TABLES], aps["W_top1"], aps["b_top1"],
                aps["W_top2"], aps["b_top2"], aps["W_top3"], aps["L0_rec_W1"], aps["L0_rec_b1"],
                aps["L0_rec_W2"], aps["L0_rec_b2"], out, gram_rows)
    r = _run(nc, [arrays], core_ids=[0])
    return r.results[0]["out_0_dram"]
```

```python
from contextlib import ExitStack

import concourse.bass as bass
from concourse import mybir

F32 = mybir.dt.float32
I32 = mybir.dt.int32
ALU = mybir.AluOpType
ACT = mybir.ActivationFunctionType


def build_tower(nc, dense, ids, tables, w_top1, b_top1, w_top2, b_top2, w_top3, w1, b1, w2, b2, out, gram_rows):
    B, DC = dense.shape
    NF = len(tables)
    K = tables[0].shape[1]
    H = w1.shape[0]
    N1, N2 = w_top1.shape[1], w_top2.shape[1]
    P = 128
    Q = P // K
    NA, NU, NT = 13, 8, 5
    NB = NU + NT
    U0, T0 = NA, NA + NU

    def n_pairs(n):
        return n * (n + 1) // 2

    PA, PB, PT = n_pairs(NA), n_pairs(NB), n_pairs(NT)
    ONE_ROW = PA
    T_ROW = PA + 1
    CUBIC_ROWS = T_ROW + PT
    ROWS = (PB, CUBIC_ROWS + NA)
    L0, L1 = 1 + NA + NU, NF
    COLS = L0 + L1
    WRAP_A, WRAP_T = NA // 2, NT // 2
    SLOT_B = NA + WRAP_A
    SLOT_T = SLOT_B + NB + NU
    SLOTS = SLOT_B + 2 * NB + WRAP_T
    SLOT_L = WRAP_A
    l_order = [(WRAP_A + i) % NA for i in range(NA)] + list(range(NA, NF))
    C_BB = 0
    C_AA = C_BB + PB
    C_B1 = C_AA + PA
    C_TT = C_B1 + 1
    C_AB = C_TT + PT
    C_UU = C_AB + NA * NB
    C_TU = C_UU + NU * NU
    RW = C_TU + NT * NU
    UB = 16
    UNITS = 4
    BT = P // Q
    TILES = B // P
    QUAD = 4
    GRAMS = NA * NF
    NG = -(-GRAMS // P)
    GC = -(-GRAMS // NG)
    VR = max(PB, CUBIC_ROWS)
    C1, C2 = N1 // P, N2 // P
    FILLS_T = BT // QUAD * 2
    VOFF = [(0, l_order[i]) for i in range(NA + NU)] + [(1, f) for f in l_order]
    NV = len(VOFF)
    assert K == 32 and NF == NA + NB and NA % 2 and NB % 2 and NT % 2 and H == P
    assert RW <= 512 and COLS == NV + 1 and NG == 3 and NA == NB and C_AA + VR <= RW

    with ExitStack() as ctx:
        def sb(name, shape, dt=F32):
            return ctx.enter_context(nc.sbuf_tensor(name, shape, dt))

        def sem(name):
            return ctx.enter_context(nc.semaphore(name))

        early = sb("early", [P, NF * NF + 2 * NF * H + RW + GRAMS + TILES * DC + C1 * B])
        moments = early[:, 0:COLS * P]
        cubic_w = sb("cubic_w", [VR, NV, H])
        pairs = sb("pairs", [P, UNITS, UB, sum(ROWS)])
        block_e = sb("block_e", [P, UNITS, UB, Q, 1 + NF])
        rows_e = sb("rows_e", [P, 2, NF * K])
        emb_t = sb("emb_t", [P, SLOTS, BT])
        late = sb("late", [P, NB * RW])
        gram_w = sb("gram_w", [GC, NG + 1, H])
        wt1 = sb("wt1", [P, 3, N1])
        wt2 = sb("wt2", [P, C1, N2])
        wt3 = sb("wt3", [P, C2])
        dense_y = sb("dense_y", [P, B])
        dense_t = dense_y[0:DC, :]
        y_all = dense_y[32:33, :]
        ids_all = sb("ids_all", [P, TILES, NF], I32)
        ids_now = sb("ids_now", [P, 2, NF], I32)
        ident = sb("ident", [P, P])
        bias1 = sb("bias1", [P, C1])
        bias2 = sb("bias2", [P, C2])
        bias_in = sb("bias_in", [P, 2])
        bias_z = sb("bias_z", [P, 2])

        ring = [ctx.enter_context(nc.psum_tensor(f"ring{i}", [P, 512], F32)) for i in range(4)]
        z_bank = [ctx.enter_context(nc.psum_tensor(f"z_bank{i}", [P, 512], F32)) for i in range(2)]
        h2_bank = [ctx.enter_context(nc.psum_tensor(f"h2_bank{i}", [P, 512], F32)) for i in range(2)]

        class Region:

            def __init__(self, base):
                self.base, self.at = base, 0

            def take(self, n):
                self.at += n
                return self.base[:, self.at - n:self.at]

            def take3(self, c, n):
                return self.take(c * n).rearrange("p (c n) -> p c n", n=n)

        pre = Region(early)
        w1_raw = pre.take(NF * NF)
        w2_raw = pre.take(H * NF)
        w2_t = pre.take(NF * H)
        w1_sym = pre.take(RW)
        gram_w_rows = pre.take(GRAMS)
        dense_rows = pre.take3(TILES, DC)
        dense_h = pre.take3(C1, B)
        assert COLS * P <= NF * NF + 2 * NF * H
        cin_a = pairs[:, 2:4].rearrange("p u b r -> p (u b r)")[:, 0:NA * RW]
        cin_b = late[:, 0:NB * RW]
        layers = Region(late)
        gram = layers.take3(NG, P)
        z_sb = layers.take3(2, P)
        h1_sum = layers.take3(C1, P)
        h1_sb = layers.take3(C1, P)
        h2_sb = layers.take3(C2, P)

        def cin(f):
            return (cin_a, f * RW) if f < NA else (cin_b, (f - NA) * RW)

        def needed(f):
            return (C_BB, C_UU) if f < NA else (C_BB, C_TU) if f < T0 else (C_AA, RW)

        pairs_flat = [pairs[:, u].rearrange("p b r -> p (b r)") for u in range(UNITS)]
        block_flat = [block_e[:, u].rearrange("p b q f -> p (b q f)") for u in range(UNITS)]
        RS = sum(ROWS)
        QS = 1 + NF
        emb = emb_t[:].rearrange("p s b -> p (s b)")

        def view(base, off, *dims):
            return bass.AP(base.tensor, base.offset + off, [list(base.ap[0])] + [list(d) for d in dims])

        ids_in = sem("ids_in")
        w1_in, w2_in, b_in, dense_in = sem("w1_in"), sem("w2_in"), sem("b_in"), sem("dense_in")
        mlp_w_in, wt1_dense_in = sem("mlp_w_in"), sem("wt1_dense_in")
        gathered = [[sem(f"gathered_{part}{slot}") for part in "ab"] for slot in range(2)]
        gram_out, gram_in = sem("gram_out"), sem("gram_in")
        y_out = sem("y_out")
        ident0, ident_ready, ids_copied = sem("ident0"), sem("ident_ready"), sem("ids_copied")
        ids_passed = sem("ids_passed")
        slot_free = sem("slot_free")
        emb_ready = sem("emb_ready")
        unit_ready = sem("unit_ready")
        w1_sym_ready, gram_rows_ready = sem("w1_sym_ready"), sem("gram_rows_ready")
        h1_summed = sem("h1_summed")
        sym_step, cin_w_ready, bias_ready = sem("sym_step"), sem("cin_w_ready"), sem("bias_ready")
        begun = sem("begun")
        ring_full = sem("ring_full")
        z_full, h2_full, y_full = sem("z_full"), sem("h2_full"), sem("y_full")
        ring_drained = sem("ring_drained")
        diagonal_ready = sem("diagonal_ready")
        z_ready, h2_ready, y_ready = sem("z_ready"), sem("h2_ready"), sem("y_ready")

        n_w2t = -(-NF // 4)
        n_dense = B // 512
        assert n_dense == 2
        n_v = -(-NV // 4)
        first_dense = 0
        first_w2t = first_dense + n_dense + C1
        first_gw = first_w2t + n_w2t + C1
        first_cin = first_gw + 1
        first_main = first_cin + NF
        first_v = first_main + FILLS_T
        FILLS_U = FILLS_T // 2
        FILLS_K = FILLS_T + C1
        assert first_main % 4 == 0 and FILLS_U % 4 == 0 and FILLS_K % 4 == 0 and n_v % 4 == 0
        CONSTS0 = UNITS + UNITS * Q + 2
        CONSTS = CONSTS0 + 2
        WARM_UP = 9
        MADE_A = 4 + Q
        MADE = MADE_A + 3 + Q + 2

        def start(k):
            if isinstance(k, int) and k == 0:
                return first_main
            return k * FILLS_K + (first_v + n_v - FILLS_K)

        def end(k):
            return first_v + n_v if isinstance(k, int) and k == 0 else start(k) + FILLS_K

        def layer1_fill(k):
            return end(k) if isinstance(k, int) and k == TILES - 1 else start(k + 1) + FILLS_U

        def batch_rows(k):
            return slice(k * P, (k + 1) * P) if isinstance(k, int) else bass.ds(k * P, P)

        N_SYM = sum(1 + 2 * (n // 2) for n in (NA, NB, NT)) + 4
        N_FIRST = sum(1 + 2 * (n // 2) for n in (NA, NB)) + NT + NB - 1
        N_SECOND = sum(2 * (n // 2) for n in (NA, NB)) + NT - 1

        def diagonal(u, h, q, part):
            lanes = slice(q * K, (q + 1) * K)
            return (view(block_flat[u][lanes], q * QS + 1 + part * NA, [Q * QS, UB], [1, NA]),
                    view(emb[lanes], (SLOT_L + part * NA) * BT + h * UB, [1, UB], [BT, NA]))

        def rotations(n, d):
            return [(0, n, 0)] if d == 0 else [(0, n - d, 0), (n - d, d, n)]

        block = ctx.enter_context(nc.Block())

        @block.sync
        def _(sp):
            sp.dma_start(ids_all[:], ids.rearrange("(t p) f -> p t f", p=P)).then_inc(ids_in, 16)
            sp.dma_start(wt1[0:DC, 2, :], w_top1[2 * P:2 * P + DC, :]).then_inc(wt1_dense_in, 16)
            sp.dma_start(w2_raw, w2.rearrange("h i l -> h (i l)")).then_inc(w2_in, 16)
            sp.dma_start(w1_raw, w1.rearrange("h i j -> h (i j)")).then_inc(w1_in, 16)
            sp.dma_start(bias_in[:, 0:1], b1.rearrange("(h a) -> h a", a=1)).then_inc(b_in, 16)
            sp.dma_start(bias_in[:, 1:2], b2.rearrange("(h a) -> h a", a=1)).then_inc(b_in, 16)
            sp.dma_start(wt1[:, 0:2, :], w_top1[0:2 * P, :].rearrange("(c p) n -> p c n", p=P)).then_inc(mlp_w_in, 16)
            sp.dma_start(wt2[:], w_top2.rearrange("(c p) n -> p c n", p=P)).then_inc(mlp_w_in, 16)
            with nc.allow_non_contiguous_dma(reason="small vectors onto the partitions"):
                sp.dma_start(wt3[:], w_top3.rearrange("(c p) a -> p (c a)", p=P)).then_inc(mlp_w_in, 16)
                sp.dma_start(bias1[:], b_top1.rearrange("(c p) -> p c", p=P)).then_inc(mlp_w_in, 16)
                sp.dma_start(bias2[:], b_top2.rearrange("(c p) -> p c", p=P)).then_inc(mlp_w_in, 16)

            def stack_gram(k):
                sp.wait_ge(ring_drained, end(k))
                src = view(moments[CUBIC_ROWS:ROWS[1]], L0 * P, [P, NF], [1, P])
                sp.dma_start(gram_rows, src).then_inc(gram_out, 16)
                sp.wait_ge(gram_out, k * 16 + 16)
                rows = gram_rows.rearrange("i l b -> (i l) b")
                for c in range(NG):
                    n = min(GC, GRAMS - c * GC)
                    sp.dma_start(gram[0:n, c, :], rows[c * GC:c * GC + n, :]).then_inc(gram_in, 16)

            stack_gram(0)
            with sp.Fori(1, TILES) as k:
                stack_gram(k)
            sp.wait_ge(y_ready, TILES)
            sp.dma_start(out.rearrange("b a -> a b"), y_all).then_inc(y_out, 16)
            sp.wait_ge(y_out, 16)

        @block.gpsimd
        def _(pool):
            nc.gpsimd.memset(ident[:], 0.0).then_inc(ident0, 1)
            pool.wait_ge(ident0, 1)
            nc.gpsimd.affine_select(out=ident[:], in_=ident[:], pattern=[[-1, P]], compare_op=ALU.not_equal,
                                    fill=1.0, base=0, channel_multiplier=1).then_inc(ident_ready, 1)
            pool.sem_inc(slot_free, 2)
            pool.wait_ge(ids_in, 16)
            with pool.Fori(0, TILES // 2) as pair:
                for slot in range(2):
                    pool.wait_ge(slot_free, pair * 2 + slot + 1)
                    nc.gpsimd.tensor_copy(ids_now[:, slot, :], ids_all[:, bass.ds(pair * 2 + slot, 1), :]).then_inc(ids_copied, 1)
                    pool.wait_ge(ids_copied, pair * 2 + slot + 1)
                    pool.sem_inc(ids_passed, 1)
                    for f in range(NF):
                        nc.gpsimd.indirect_dma_start(
                            out=rows_e[:, slot, f * K:(f + 1) * K], out_offset=None, in_=tables[f],
                            in_offset=bass.IndirectOffsetOnAxis(ap=ids_now[:, slot, f:f + 1], axis=0),
                        ).then_inc(gathered[slot][0 if f < NA else 1], 16)

        @block.vector
        def _(dve):
            def add(dst, a, b, signal):
                nc.vector.tensor_tensor(dst, a, b, ALU.add).then_inc(signal, 1)

            def copy(dst, src, signal):
                nc.vector.tensor_copy(dst, src).then_inc(signal, 1)

            def ones_row(u):
                nc.vector.memset(pairs[:, u, :, PB + ONE_ROW:PB + ONE_ROW + 1], 1.0).then_inc(unit_ready, 1)

            for u in range(UNITS):
                nc.vector.memset(block_e[:, u], 0.0).then_inc(unit_ready, 1)
            dve.wait_ge(unit_ready, UNITS)
            for u in range(UNITS):
                for q in range(Q):
                    nc.vector.memset(block_e[q * K:(q + 1) * K, u, :, q, 0:1], 1.0).then_inc(unit_ready, 1)
            for u in range(2):
                ones_row(u)

            dve.wait_ge(w1_in, 16)
            dve.wait_ge(b_in, 32)
            for at, n, f0 in ((C_BB, NB, U0), (C_AA, NA, 0), (C_TT, NT, T0)):
                copy(view(w1_sym, at, [1, n]), view(w1_raw, f0 * (NF + 1), [NF + 1, n]), w1_sym_ready)
                for d in range(1, n // 2 + 1):
                    for i, m, wrap in rotations(n, d):
                        a, b = f0 + i, f0 + i + d - wrap
                        add(view(w1_sym, at + d * n + i, [1, m]), view(w1_raw, a * NF + b, [NF + 1, m]),
                            view(w1_raw, b * NF + a, [NF + 1, m]), w1_sym_ready)
            copy(view(w1_sym, C_B1, [1, 1]), bias_in[:, 0:1], w1_sym_ready)
            add(view(w1_sym, C_AB, [NB, NA], [1, NB]), view(w1_raw, U0, [NF, NA], [1, NB]),
                view(w1_raw, U0 * NF, [1, NA], [NF, NB]), w1_sym_ready)
            add(view(w1_sym, C_TU, [NU, NT], [1, NU]), view(w1_raw, T0 * NF + U0, [NF, NT], [1, NU]),
                view(w1_raw, U0 * NF + T0, [1, NT], [NF, NU]), w1_sym_ready)
            copy(view(w1_sym, C_UU, [NU, NU], [1, NU]), view(w1_raw, U0 * NF + U0, [NF, NU], [1, NU]), w1_sym_ready)
            first = NA - WRAP_A
            copy(view(gram_w_rows, 0, [NF, NA], [1, first]), view(w1_raw, WRAP_A, [NF, NA], [1, first]), gram_rows_ready)
            copy(view(gram_w_rows, first, [NF, NA], [1, WRAP_A]), view(w1_raw, 0, [NF, NA], [1, WRAP_A]), gram_rows_ready)
            add(view(gram_w_rows, NA, [NF, NA], [1, NB]), view(w1_raw, U0, [NF, NA], [1, NB]),
                view(w1_raw, U0 * NF, [1, NA], [NF, NB]), gram_rows_ready)
            nc.vector.tensor_scalar(bias_z[:], bias_in[:], float(K), None, ALU.mult).then_inc(bias_ready, 1)

            def fold(dst, src, signal):
                add(dst, dst, src, signal)

            def cin_view(f, column, *dims):
                part, at = cin(f)
                return view(part, at + column, *dims)

            def first_pass(sig):
                for n, at, own0, l0, nl, ls, xs in ((NA, C_AA, 0, U0, NB, 1, NB), (NB, C_BB, U0, 0, NA, NB, 1)):
                    for d in range(n // 2 + 1):
                        for i, m, wrap in rotations(n, d):
                            j = i + d - wrap
                            fold(cin_view(l0, at + d * n + i, [RW, nl], [1, m]),
                                 cin_view(own0 + j, C_AB + i * xs, [ls, nl], [RW + xs, m]), sig)
                for d in range(NT):
                    fold(tu_cell(d), cin_view(T0 + d, C_TU, [1, NU], [RW + NU, NT - d]), sig)
                for e in range(1, NB):
                    u_lo, u_hi = max(0, NU - e), min(NU - 1, NB - 1 - e)
                    at = e * NB + u_lo if e <= NB // 2 else (NB - e) * NB + e + u_lo
                    m = u_hi - u_lo + 1
                    fold(cin_view(U0, C_BB + at, [RW, NU], [1, m]),
                         cin_view(U0 + e + u_lo, C_UU + u_lo, [NU, NU], [RW + 1, m]), sig)

            def tu_cell(d):
                at = d * NB + NU if d <= NB // 2 else (NB - d) * NB + NU + d
                return cin_view(U0, C_BB + at, [RW, NU], [1, NT - d])

            def second_pass(sig):
                for n, at, own0, l0, nl, ls, xs in ((NA, C_AA, 0, U0, NB, 1, NB), (NB, C_BB, U0, 0, NA, NB, 1)):
                    for d in range(1, n // 2 + 1):
                        for i, m, wrap in rotations(n, d):
                            j = i + d - wrap
                            fold(cin_view(l0, at + d * n + i, [RW, nl], [1, m]),
                                 cin_view(own0 + i, C_AB + j * xs, [ls, nl], [RW + xs, m]), sig)
                for d in range(1, NT):
                    fold(tu_cell(d), cin_view(T0, C_TU + d * NU, [1, NU], [RW + NU, NT - d]), sig)

            def transpose_rows(slot, dst, f, n, signal):
                nc.vector.transpose(view(emb, dst * BT, [1, n * BT]),
                                    rows_e[:, slot, f * K:(f + n) * K]).then_inc(signal, 1)

            def make_pairs(u, h, at, n, s, first=0, count=UB):
                b0 = h * UB + first
                nc.vector.tensor_tensor(
                    view(pairs_flat[u], first * RS + at, [RS, count], [n, n // 2 + 1], [1, n]),
                    view(emb, s * BT + b0, [1, count], [0, n // 2 + 1], [BT, n]),
                    view(emb, s * BT + b0, [1, count], [BT, n // 2 + 1], [BT, n]),
                    ALU.mult).then_inc(unit_ready, 1)

            def make_a(slot, gathers, made, tiles, free):
                dve.wait_ge(gathered[slot][0], gathers * NA)
                dve.wait_ge(unit_ready, made)
                transpose_rows(slot, 0, 0, NA, emb_ready)
                transpose_rows(slot, NA, 0, WRAP_A, emb_ready)
                dve.wait_ge(emb_ready, tiles * 5 + 2)
                for h in range(2):
                    u = slot * 2 + h
                    if free is not None:
                        dve.wait_ge(begun, free + h)
                    make_pairs(u, h, PB, NA, 0)
                    copy(view(pairs_flat[u], PB + CUBIC_ROWS, [RS, UB], [1, NA]),
                         view(emb, h * UB, [1, UB], [BT, NA]), unit_ready)
                for q in range(Q):
                    copy(*diagonal(slot * 2 + 1, 1, q, 0), unit_ready)

            def make_b(slot, gathers, tiles):
                dve.wait_ge(gathered[slot][1], gathers * NB)
                transpose_rows(slot, SLOT_B, U0, NB, emb_ready)
                transpose_rows(slot, SLOT_B + NB, U0, NU, emb_ready)
                dve.wait_ge(emb_ready, tiles * 5 + 4)
                u = slot * 2
                make_pairs(u, 0, 0, NB, SLOT_B, 0, UB // 2)
                transpose_rows(slot, SLOT_T, T0, NT, emb_ready)
                transpose_rows(slot, SLOT_T + NT, T0, WRAP_T, slot_free)
                dve.wait_ge(emb_ready, tiles * 5 + 5)
                dve.wait_ge(slot_free, tiles + 3)
                make_pairs(u, 0, PB + T_ROW, NT, SLOT_T)
                make_pairs(u, 0, 0, NB, SLOT_B, UB // 2, UB // 2)
                for q in range(Q):
                    copy(*diagonal(u + 1, 1, q, 1), unit_ready)
                make_pairs(u + 1, 1, 0, NB, SLOT_B)
                make_pairs(u + 1, 1, PB + T_ROW, NT, SLOT_T)

            def add_dense(k):
                for m in range(C1):
                    dve.wait_ge(ring_full, layer1_fill(k) + (m + 1))
                    nc.vector.tensor_tensor(h1_sum[:, m, :], ring[m][:, 0:P], dense_h[:, m, batch_rows(k)],
                                            ALU.add).then_inc(h1_summed, 1)

            make_a(0, 16, CONSTS0, 0, None)
            make_b(0, 16, 0)

            dve.wait_ge(ring_drained, first_cin + NF)
            first_pass(sym_step)
            dve.wait_ge(sym_step, N_FIRST)
            second_pass(cin_w_ready)
            dve.wait_ge(ring_drained, first_v + n_v)
            for u in range(2, UNITS):
                ones_row(u)
            make_a(1, 16, CONSTS + MADE, 1, None)
            make_b(1, 16, 1)
            add_dense(0)

            with dve.Fori(1, TILES // 2) as pair:
                for slot in range(2):
                    k = pair * 2 + slot
                    make_a(slot, pair * 16 + 16, pair * (2 * MADE) + (CONSTS + slot * MADE),
                           k, pair * 6 + (3 * slot - 4))
                    make_b(slot, pair * 16 + 16, k)
                    add_dense(k - 1)
            add_dense(TILES - 1)

        @block.tensor
        def _(pe):
            fill = [0]

            def ring_bank():
                n = fill[0]
                fill[0] += 1
                if n >= 4:
                    pe.wait_ge(ring_drained, n - 3)
                return ring[n % 4]

            pe.wait_ge(ident_ready, 1)
            for _ in range(WARM_UP):
                nc.tensor.matmul(ring[3][:, 0:P], ident[:], ident[:], start=True, stop=True)
            pe.wait_ge(dense_in, 16)
            for c in range(n_dense):
                bank = ring_bank()
                for t in range(4):
                    mm = nc.tensor.transpose(bank[0:DC, t * P:(t + 1) * P], dense_rows[:, c * 4 + t, :], ident[:])
                mm.then_inc(ring_full, 1)

            def layer1_dense(c):
                pe.wait_ge(wt1_dense_in, 16)
                pe.wait_ge(ring_drained, first_dense + c + 1)
                for m in range(C1):
                    bank = ring_bank()
                    nc.tensor.matmul(bank[:, :], wt1[0:DC, 2, m * P:(m + 1) * P], dense_t[:, c * 512:(c + 1) * 512],
                                     start=True, stop=True).then_inc(ring_full, 1)

            layer1_dense(0)
            pe.wait_ge(w2_in, 16)
            w2v = w2_raw.rearrange("h (i l) -> h i l", l=NF)
            for c in range(n_w2t):
                bank = ring_bank()
                for f in range(4 * c, min(4 * c + 4, NF)):
                    mm = nc.tensor.transpose(bank[:, (f % 4) * H:(f % 4 + 1) * H], w2v[:, :, f], ident[:])
                mm.then_inc(ring_full, 1)
            layer1_dense(1)
            pe.wait_ge(gram_rows_ready, 3)
            pe.wait_ge(w1_sym_ready, N_SYM)
            bank = ring_bank()
            for c in range(NG):
                n = min(GC, GRAMS - c * GC)
                nc.tensor.transpose(bank[0:n, c * H:(c + 1) * H], gram_w_rows[:, c * GC:c * GC + n], ident[:])
            nc.tensor.transpose(bank[0:PB, NG * H:(NG + 1) * H], w1_sym[:, C_BB:C_BB + PB], ident[:]).then_inc(ring_full, 1)
            pe.wait_ge(ring_drained, first_w2t + n_w2t)
            for f in range(NF):
                bank = ring_bank()
                c0, c1 = needed(f)
                nc.tensor.matmul(bank[:, 0:c1 - c0], w2_t[:, f * H:(f + 1) * H], w1_sym[:, c0:c1],
                                 start=True, stop=True).then_inc(ring_full, 1)

            def transpose_cubic():
                pe.wait_ge(cin_w_ready, N_SECOND)
                for c in range(n_v):
                    n = first_v + c
                    bank = ring[n % 4]
                    pe.wait_ge(ring_drained, n - 3)
                    for v in range(4 * c, min(4 * c + 4, NV)):
                        g, f = VOFF[v]
                        part, at = cin(f)
                        at += C_BB if g == 0 else C_AA
                        mm = nc.tensor.transpose(bank[0:VR, (v % 4) * H:(v % 4 + 1) * H], part[:, at:at + VR], ident[:])
                    mm.then_inc(ring_full, 1)

            def unit_moments(at, off, made, h, u):
                for n in range(off, off + FILLS_U):
                    quad, g = (n - off) // 2, n % 2
                    if h == 0 and (quad, g) in ((0, 0), (0, 1), (UB // QUAD // 2, 0)):
                        pe.wait_ge(unit_ready, made + (MADE_A + 1 + (g if quad == 0 else 2)))
                    if h == 1 and n == off:
                        pe.wait_ge(unit_ready, made + MADE)
                    bank = ring[n % 4]
                    pe.wait_ge(ring_drained, at + (n - 3))
                    cols = L0 if g == 0 else L1
                    for b in range(quad * QUAD, (quad + 1) * QUAD):
                        to = b % QUAD * Q * cols
                        mm = nc.tensor.matmul(bank[0:ROWS[g], to:to + Q * cols],
                                              pairs[:, u, b, 0:PB] if g == 0 else pairs[:, u, b, PB:RS],
                                              view(block_flat[u], b * Q * QS + g, [QS, Q], [1, cols]),
                                              start=True, stop=True)
                        if n == off and b == 0:
                            mm.then_inc(begun, 1)
                    mm.then_inc(ring_full, 1)

            def sums(k):
                first = isinstance(k, int) and k == 0
                if not first:
                    pe.wait_ge(ring_drained, end(k))
                for v in range(NV):
                    if first and v % 4 == 0:
                        pe.wait_ge(ring_drained, first_v + v // 4 + 1)
                    g, f = VOFF[v]
                    rows = PB if g == 0 else (CUBIC_ROWS if f >= T0 else T_ROW)
                    mm = nc.tensor.matmul(z_bank[1][:, 0:P], cubic_w[0:rows, v, :], moments[0:rows, (v + 1) * P:(v + 2) * P],
                                          start=(v == 0), stop=(v == NV - 1))
                    if v == 0:
                        mm.then_inc(begun, 1)
                mm.then_inc(z_full, 1)
                nc.tensor.matmul(z_bank[0][:, 0:P], gram_w[0:PB, NG, :], moments[0:PB, 0:P], start=True, stop=False)
                pe.wait_ge(gram_in, k * (16 * NG) + 16 * NG)
                for c in range(NG):
                    rows = min(GC, GRAMS - c * GC)
                    mm = nc.tensor.matmul(z_bank[0][:, 0:P], gram_w[0:rows, c, :], gram[0:rows, c, :],
                                          start=False, stop=(c == NG - 1))
                mm.then_inc(z_full, 1)
                if not (isinstance(k, int) and k == 0):
                    layer3(k - 1)

            def layer1(k):
                steps = [(m, part) for m in range(C1) for part in range(2)]
                if isinstance(k, int) and k == TILES - 1:
                    steps.sort(key=lambda step: step[1])
                for m, part in steps:
                    if m == 0:
                        pe.wait_ge(z_ready, k * 2 + (part + 1))
                    if part == 0:
                        pe.wait_ge(ring_drained, layer1_fill(k) + (m - 3))
                    mm = nc.tensor.matmul(ring[m][:, 0:P], wt1[:, 1 - part, m * P:(m + 1) * P], z_sb[:, 1 - part, :],
                                          start=(part == 0), stop=(part == 1))
                    if part == 1:
                        mm.then_inc(ring_full, 1)

            def layer2(k):
                for c in range(C1):
                    pe.wait_ge(ring_drained, layer1_fill(k) + (c + 1))
                    for m in range(C2):
                        mm = nc.tensor.matmul(h2_bank[m][:, 0:P], wt2[:, c, m * P:(m + 1) * P], h1_sb[:, c, :],
                                              start=(c == 0), stop=(c == C1 - 1))
                        if c == C1 - 1:
                            mm.then_inc(h2_full, 1)

            def layer3(k):
                for c in range(C2):
                    pe.wait_ge(h2_ready, k * C2 + (c + 1))
                    mm = nc.tensor.matmul(h2_bank[0][32:33, 0:P], wt3[:, c:c + 1], h2_sb[:, c, :],
                                          start=(c == 0), stop=(c == C2 - 1))
                mm.then_inc(y_full, 1)

            def moments_and_layers(k, slot):
                pe.wait_ge(diagonal_ready, k * (2 * Q) + 2 * Q)
                for j in range(2):
                    unit_moments(start(k), j * (FILLS_U + C1), k * MADE + CONSTS, j, slot * 2 + j)
                    (layer1, layer2)[j](k - 1)
                sums(k)

            pe.wait_ge(mlp_w_in, 16 * 5)
            pe.wait_ge(diagonal_ready, 2 * Q)
            for j in range(2):
                unit_moments(start(0), j * FILLS_U, CONSTS0, j, j)
            transpose_cubic()
            sums(0)
            moments_and_layers(1, 1)
            with pe.Fori(1, TILES // 2) as pair:
                for slot in range(2):
                    moments_and_layers(pair * 2 + slot, slot)
            layer1(TILES - 1)
            layer2(TILES - 1)
            layer3(TILES - 1)

        @block.scalar
        def _(act):
            act.dma_start(dense_rows, dense.rearrange("(t p) c -> p t c", p=P)).then_inc(dense_in, 16)

            def drain(n, dst, rows, cols):
                act.wait_ge(ring_full, n + 1)
                nc.scalar.activation(dst, ring[n % 4][0:rows, 0:cols], ACT.Copy).then_inc(ring_drained, 1)

            n = 0
            for c in range(n_dense):
                drain(n, dense_t[:, c * 512:(c + 1) * 512], DC, 512)
                n += 1
            for m in range(C1):
                drain(n, dense_h[:, m, 0:512], P, 512)
                n += 1
            for c in range(n_w2t):
                w = min(4, NF - 4 * c) * H
                drain(n, w2_t[:, 4 * c * H:4 * c * H + w], P, w)
                n += 1
            for m in range(C1):
                drain(n, dense_h[:, m, 512:1024], P, 512)
                n += 1
            act.wait_ge(ring_full, n + 1)
            for c in range(NG):
                rows = min(GC, GRAMS - c * GC)
                nc.scalar.activation(gram_w[0:rows, c, :], ring[n % 4][0:rows, c * H:(c + 1) * H], ACT.Copy)
            nc.scalar.activation(gram_w[0:PB, NG, :], ring[n % 4][0:PB, NG * H:(NG + 1) * H], ACT.Copy).then_inc(ring_drained, 1)
            n += 1
            for f in range(NF):
                part, at = cin(f)
                c0, c1 = needed(f)
                drain(n, part[:, at + c0:at + c1], P, c1 - c0)
                n += 1

            def first_diagonal(k, slot):
                for part in range(2):
                    act.wait_ge(emb_ready, k * 5 + (part + 2))
                    for q in range(Q):
                        nc.scalar.activation(*diagonal(slot * 2, 0, q, part), ACT.Copy).then_inc(diagonal_ready, 1)

            def unit_moments(at, off, h):
                for n in range(off, off + FILLS_U):
                    quad, g = (n - off) // 2, n % 2
                    cols, rows = (L0, L1)[g], ROWS[g]
                    act.wait_ge(ring_full, at + (n + 1))
                    dst = view(moments[0:rows], g * L0 * P + h * UB + quad * QUAD, [BT, Q], [P, cols], [1, QUAD])
                    src = view(ring[n % 4][0:rows, :], 0, [cols, Q], [1, cols], [Q * cols, QUAD])
                    nc.scalar.activation(dst, src, ACT.Copy).then_inc(ring_drained, 1)

            def sums(k):
                for c in (1, 0):
                    act.wait_ge(z_full, k * 2 + (2 - c))
                    nc.scalar.activation(z_sb[:, c, :], z_bank[c][:, 0:P], ACT.Identity,
                                         bias=bias_z[:, c:c + 1]).then_inc(z_ready, 1)
                if not (isinstance(k, int) and k == 0):
                    layer3(k - 1)

            def layer1(k):
                for m in range(C1):
                    act.wait_ge(h1_summed, k * C1 + (m + 1))
                    nc.scalar.activation(h1_sb[:, m, :], h1_sum[:, m, :], ACT.Relu,
                                         bias=bias1[:, m:m + 1]).then_inc(ring_drained, 1)

            def layer2(k):
                for m in range(C2):
                    act.wait_ge(h2_full, k * C2 + (m + 1))
                    nc.scalar.activation(h2_sb[:, m, :], h2_bank[m][:, 0:P], ACT.Relu,
                                         bias=bias2[:, m:m + 1]).then_inc(h2_ready, 1)

            def layer3(k):
                act.wait_ge(y_full, k + 1)
                nc.scalar.activation(y_all[:, batch_rows(k)], h2_bank[0][32:33, 0:P],
                                     ACT.Copy).then_inc(y_ready, 1)

            def tile_after(k, slot):
                first_diagonal(k, slot)
                sums(k - 1)
                for j in range(2):
                    unit_moments(start(k), j * (FILLS_U + C1), j)
                    (layer1, layer2)[j](k - 1)

            act.wait_ge(bias_ready, 1)
            act.wait_ge(mlp_w_in, 16 * 5)
            first_diagonal(0, 0)
            for j in range(2):
                unit_moments(start(0), j * FILLS_U, j)
            cw = cubic_w[:].rearrange("p v h -> p (v h)")
            for c in range(n_v):
                w = min(4, NV - 4 * c) * H
                drain(first_v + c, cw[:, 4 * c * H:4 * c * H + w], VR, w)
            tile_after(1, 1)
            with act.Fori(1, TILES // 2) as pair:
                for slot in range(2):
                    tile_after(pair * 2 + slot, slot)
            sums(TILES - 1)
            layer1(TILES - 1)
            layer2(TILES - 1)
            layer3(TILES - 1)


_TABLES = [f"tbl_{f}" for f in range(26)]
_INS = ["dense_ctx", "ids"] + _TABLES + ["W_top1", "b_top1", "W_top2", "b_top2", "W_top3",
                                         "L0_rec_W1", "L0_rec_b1", "L0_rec_W2", "L0_rec_b2"]


def kernel(**inputs):
    import numpy as _np
    import concourse.bacc as _bacc
    from concourse import mybir as _mybir
    from concourse.bass_utils import run_bass_kernel_spmd as _run

    nc = _bacc.Bacc("TRN2", target_bir_lowering=False, num_devices=1)
    arrays, aps = {}, {}
    for name in _INS:
        a = _np.ascontiguousarray(inputs[name])
        arrays[f"in_{name}_dram"] = a
        aps[name] = nc.dram_tensor(f"in_{name}_dram", a.shape, _mybir.dt.from_np(a.dtype), kind="ExternalInput").ap()
    out = nc.dram_tensor("out_0_dram", (inputs["dense_ctx"].shape[0], 1), _mybir.dt.float32, kind="ExternalOutput").ap()
    gram_rows = nc.dram_tensor("gram_rows", (13, 26, 128), _mybir.dt.float32, kind="Internal").ap()
    build_tower(nc, aps["dense_ctx"], aps["ids"], [aps[t] for t in _TABLES], aps["W_top1"], aps["b_top1"],
                aps["W_top2"], aps["b_top2"], aps["W_top3"], aps["L0_rec_W1"], aps["L0_rec_b1"],
                aps["L0_rec_W2"], aps["L0_rec_b2"], out, gram_rows)
    r = _run(nc, [arrays], core_ids=[0])
    return r.results[0]["out_0_dram"]
```
